# Optimizing a Trainium2 kernel written in Bass

```python
import numpy as np
import jax
import jax.numpy as jnp

def _softmax(x, axis=-1):
    return jax.nn.softmax(x, axis=axis)

def _gelu(x):
    return jax.nn.gelu(x, approximate=True)

def _silu(x):
    return jax.nn.silu(x)

def _sigmoid(x):
    return jax.nn.sigmoid(x)

def _layernorm(x, axis=-1, eps=1e-05):
    m = jnp.mean(x, axis=axis, keepdims=True)
    v = jnp.var(x, axis=axis, keepdims=True)
    return (x - m) / jnp.sqrt(v + eps)

def _scatter_add(tgt, idx, src, axis=0):
    return tgt.at[idx].add(src)

def _segment_sum(src, seg, n):
    return jax.ops.segment_sum(src, seg, n)
kernel_name = 'mk_seq_postln_d1_jaxref_r4_a0f94d'

def setup_inputs(seed: int=0):
    np.random.seed(seed)
    _w = jnp.asarray

    def _L0_attn_setup():
        import math
        import jax, jax.numpy as jnp
        import numpy as np
        D = 256
        NH = 16
        DH = D // NH

        def _rope(q, k, base=10000.0):
            half = q.shape[-1] // 2
            freqs = jnp.arange(half, dtype=q.dtype) / half
            theta = 1.0 / base ** freqs
            t = jnp.arange(q.shape[-2], dtype=q.dtype)
            ang = t[:, None] * theta[None, :]
            cos = jnp.cos(ang)[None, None, :, :]
            sin = jnp.sin(ang)[None, None, :, :]

            def rot(x):
                x1, x2 = (x[..., :half], x[..., half:])
                return jnp.concatenate([x1 * cos - x2 * sin, x1 * sin + x2 * cos], axis=-1)
            return (rot(q), rot(k))
        key = jax.random.key(seed)
        k1, k2, k3 = jax.random.split(key, 3)
        x = jax.random.normal(k1, (2, 512, D), dtype=jnp.float32)
        s = 1.0 / math.sqrt(D)
        W_qkv = jax.random.normal(k2, (D, 3 * D), dtype=jnp.float32) * s
        W_o = jax.random.normal(k3, (D, D), dtype=jnp.float32) * s
        return {'x': x, 'W_qkv': W_qkv, 'W_o': W_o}
    _L0_attn_in = _L0_attn_setup()

    def _L0_ffn_setup():
        import jax, jax.numpy as jnp
        import numpy as np
        IN_DIM = 256
        OUT_DIM = 256
        NUM_EXPERTS = 8
        TOP_K = 2
        key = jax.random.key(seed)
        ks = jax.random.split(key, 5)
        s = 1.0 / np.sqrt(IN_DIM)
        x = jax.random.normal(ks[0], (4, 512, IN_DIM), dtype=jnp.float32)
        Wg = jax.random.uniform(ks[1], (IN_DIM, NUM_EXPERTS), jnp.float32, -s, s)
        bg = jnp.zeros((NUM_EXPERTS,), jnp.float32)
        We = jax.random.uniform(ks[2], (NUM_EXPERTS, OUT_DIM, IN_DIM), jnp.float32, -s, s)
        be = jax.random.uniform(ks[3], (NUM_EXPERTS, OUT_DIM), jnp.float32, -s, s)
        return {'x': x, 'Wg': Wg, 'bg': bg, 'We': We, 'be': be}
    _L0_ffn_in = _L0_ffn_setup()
    _d = {'L0_attn_x': _L0_attn_in['x'], 'L0_attn_W_qkv': _L0_attn_in['W_qkv'], 'L0_attn_W_o': _L0_attn_in['W_o'], 'L0_ffn_Wg': _L0_ffn_in['Wg'], 'L0_ffn_bg': _L0_ffn_in['bg'], 'L0_ffn_We': _L0_ffn_in['We'], 'L0_ffn_be': _L0_ffn_in['be']}
    _x0 = _d['L0_attn_x']
    _d['L0_attn_x'] = jax.random.normal(jax.random.fold_in(jax.random.key(seed), 1), (16, 1024, 256), dtype=_x0.dtype)
    del _x0
    return _d

def reference(L0_attn_x, L0_attn_W_qkv, L0_attn_W_o, L0_ffn_Wg, L0_ffn_bg, L0_ffn_We, L0_ffn_be):

    def _L0_attn_ref(x, W_qkv, W_o):
        import math
        import jax, jax.numpy as jnp
        import numpy as np
        D = 256
        NH = 16
        DH = D // NH

        def _rope(q, k, base=10000.0):
            half = q.shape[-1] // 2
            freqs = jnp.arange(half, dtype=q.dtype) / half
            theta = 1.0 / base ** freqs
            t = jnp.arange(q.shape[-2], dtype=q.dtype)
            ang = t[:, None] * theta[None, :]
            cos = jnp.cos(ang)[None, None, :, :]
            sin = jnp.sin(ang)[None, None, :, :]

            def rot(x):
                x1, x2 = (x[..., :half], x[..., half:])
                return jnp.concatenate([x1 * cos - x2 * sin, x1 * sin + x2 * cos], axis=-1)
            return (rot(q), rot(k))
        B, T, d = x.shape
        qkv = x @ W_qkv
        q, k, v = jnp.split(qkv, 3, axis=-1)
        q = q.reshape(B, T, NH, DH).transpose(0, 2, 1, 3)
        k = k.reshape(B, T, NH, DH).transpose(0, 2, 1, 3)
        v = v.reshape(B, T, NH, DH).transpose(0, 2, 1, 3)
        q, k = _rope(q, k)
        att = jnp.einsum('bhtd,bhsd->bhts', q, k) / math.sqrt(DH)
        mask = jnp.triu(jnp.full((T, T), -jnp.inf, dtype=att.dtype), 1)
        att = att + mask
        w = jax.nn.softmax(att, axis=-1)
        y = jnp.einsum('bhts,bhsd->bhtd', w, v)
        y = y.transpose(0, 2, 1, 3).reshape(B, T, d)
        return y @ W_o

    def _L0_ffn_ref(x, Wg, bg, We, be):
        import jax, jax.numpy as jnp
        import numpy as np
        IN_DIM = 256
        OUT_DIM = 256
        NUM_EXPERTS = 8
        TOP_K = 2
        gate = jax.nn.softmax(x @ Wg + bg, axis=-1)
        topk_vals, topk_idx = jax.lax.top_k(gate, TOP_K)
        onehot = jax.nn.one_hot(topk_idx, NUM_EXPERTS, dtype=gate.dtype)
        gate_sparse = jnp.einsum('bsk,bske->bse', topk_vals, onehot)
        gate_sparse = gate_sparse / jnp.sum(gate_sparse, axis=-1, keepdims=True)
        y = jnp.einsum('bsi,eoi->bseo', x, We) + be[None, None, :, :].transpose(0, 1, 2, 3)
        out = jnp.einsum('bseo,bse->bso', y, gate_sparse)
        return out
    x = L0_attn_x
    x = _layernorm(x + _L0_attn_ref(x, L0_attn_W_qkv, L0_attn_W_o), axis=-1)
    x = _layernorm(x + _L0_ffn_ref(x, L0_ffn_Wg, L0_ffn_bg, L0_ffn_We, L0_ffn_be), axis=-1)
    return x

_drawn_inputs = setup_inputs


def setup_inputs(seed=0):
    import zlib

    import numpy as np

    out = dict(_drawn_inputs(seed))
    spreads = {'L0_ffn_bg': (0.0, 0.1)}
    factors = {}
    for name, (base, spread) in spreads.items():
        noise = np.random.default_rng([zlib.crc32(name.encode()), seed]).standard_normal(out[name].shape)
        drawn = base * np.exp(spread * noise) if base else spread * noise
        out[name] = jnp.asarray(drawn.astype(out[name].dtype))
    for name, factor in factors.items():
        out[name] = (out[name] * factor).astype(out[name].dtype)
    return out
```

```python
from contextlib import ExitStack

import numpy as np

import concourse.bass as bass
from concourse import mybir

F32 = mybir.dt.float32
F32R = mybir.dt.float32r
BF16 = mybir.dt.bfloat16
I32 = mybir.dt.int32
ALU = mybir.AluOpType
ACT = mybir.ActivationFunctionType
AX = mybir.AxisListType

P = 128
B, T, D = 16, 1024, 256
NH = 16
DH = D // NH
NE = 8
TILES = T // P
CH = 512
KT = D // P
QUAD = 4
SLOTS = NH // QUAD
ITEMS = 12
ITEM = [(kb, qc) for qc in range(T // CH) for kb in range(CH // P * (qc + 1))]
HALF = P // DH
TERMS = ((0, 0), (0, 1), (1, 0), (1, 1), (0, 2), (2, 0))
ROWS = len(TERMS) * DH
MROWS = ROWS + 3
VW = DH + 1
VQ = TILES * QUAD * VW + 32 - VW
EPS = 1e-5
FAR = -1e38
SENTINEL = 3e38
MAGIC = 0x5F3759DF
NB = 3
DMA = 16


BITEM = [(qt, kc) for kc in range(T // CH) for qt in range(CH // P * kc, TILES)]
LOADS = 2 * len(TERMS) * DMA
W_LOADS = 9
CONST_P, CONST_V = 5, 4
SWAP = [(i // DH) * DH + (i + DH // 2) % DH for i in range(32)]
LAST_B = ("B", SLOTS - 1, ITEMS - 1, QUAD - 1)


def score_width(kb, qc):
    return max(0, kb * P - qc * CH)


SEGMENTS = ("pre", "first", "mid", "last", "post")
NMID = B - 2


def plan(seg):
    ahead = seg in ("pre", "first", "mid")
    attend = seg in ("first", "mid", "last")
    behind = seg in ("mid", "last", "post")
    at = [[] for _ in range(SLOTS * ITEMS)]

    if ahead and seg != "pre":
        at[0] += [("XL", 0), ("XL", 1)]
        at[1] += [("XT", 0), ("XL", 2), ("XT", 1), ("XL", 3)]
        at[2] += [("XT", 2), ("XT", 3)]
        for s in range(NH // HALF):
            for k in range(4):
                n = 3 + 14 * s + 2 * k
                at[n].append(("QK", s, k))
                at[n + 1].append(("ROPE", s, k))
                at[n + 3].append(("SPLIT", s, k))
        for j in range(TILES // 2):
            at[12 + j].append(("VP", j))
        for s in range(SLOTS - 1):
            at[(18, 26, 38)[s]].append(("VCOPY", s))
    if attend:
        at[2].append(("VCOPY", SLOTS - 1))
    if behind:
        at[1].append(("YT", SLOTS - 1, 1))
        for g, (moe0, moe1) in enumerate(((13, 27), (34, 44))):
            o = 3 + 2 * g
            at[0].append(("XR", g))
            at[o - 1] += [("HT", g, kt) for kt in range(KT)]
            at[o] += [("WO", g, tp) for tp in range(2)]
            at[o + 1].append(("N1", g))
            at[o + 2].append(("N1A", g))
            o3 = (6, 28)[g]
            at[o3] += [("ZT", g, kt) for kt in range(KT)]
            at[o3 + 1].append(("GL", g))
            at[o3 + 2].append(("GLT", g))
            at[o3 + 3].append(("GA", g))
            at[o3 + 4].append(("GB", g))
            at[o3 + 5].append(("GT", g))
            at[o3 + 5] += [("BE", g, tp) for tp in range(2)] if g else []
            if not g:
                at[o3 + 6] += [("BE", g, tp) for tp in range(2)]
            jobs = [("MOE", g, t, c) for t in range(4) for c in range(NE // 2)]
            for n, job in enumerate(jobs):
                at[moe0 + n * (moe1 - moe0) // len(jobs)].append(job)
            at[moe1 + 1].append(("N2", g))
            at[moe1 + 2].append(("N2A", g))
    if attend:
        for s in range(SLOTS):
            at[ITEMS * s + 6].append(("YT", s, 0))
            if s + 1 < SLOTS:
                at[ITEMS * s + ITEMS + 1].append(("YT", s, 1))
    bslots = {"pre": (), "first": (0, 1, 2, 3), "mid": (0, 1, 2, 3), "last": (0, 1), "post": ()}[seg]
    for s in bslots:
        if s < SLOTS - 1:
            at[ITEMS * s + ITEMS + 1].append(("MT", s))
    if seg == "mid" or seg == "last":
        at[1].append(("MT", SLOTS - 1))

    out = []
    if seg == "pre":
        out += [("XL", 0), ("XL", 1), ("XT", 0), ("XL", 2), ("XT", 1), ("XL", 3), ("XT", 2), ("XT", 3)]
        for s in range(NH // HALF):
            for k in range(4):
                out += [("QK", s, k), ("ROPE", s, k), ("SPLIT", s, k)]
            if s == 0:
                out += [("LOAD", 0), ("LOAD", 1)]
        out += [("VP", j) for j in range(TILES // 2)] + [("VCOPY", s) for s in range(SLOTS - 1)]
        out += [("LOAD", 2)]
        for s in range(2):
            out += [("B", s, it, hh) for it in range(ITEMS) for hh in range(QUAD)]
            out += [("MT", s)]
        return out
    for n in range(SLOTS * ITEMS):
        s, it = divmod(n, ITEMS)
        if attend:
            if it == 2 and (ahead or s == 0):
                out.append(("LOAD", s))
            out.append(("ST", n, 0))
            bj = [("B", s, it, hh) for hh in range(QUAD)] if s in bslots else []
            out += bj[:2]
            out.append(("ST", n, 1))
        ex = at[n]
        half = (len(ex) + 1) // 2
        out += ex[:half]
        if attend:
            out += bj[2:]
        out += ex[half:]
        if attend and n:
            out += [("PV", n - 1)]
            if (n - 1) % ITEMS in (3, ITEMS - 1):
                out.append(("YE", (n - 1) // ITEMS, int((n - 1) % ITEMS != 3)))
        if n == 0 and behind:
            out += [("PV", SLOTS * ITEMS - 1), ("YE", SLOTS - 1, 1)]
    return out


BANKED = ("XT", "QK", "VP", "YT", "HT", "WO", "ZT", "GL", "GLT", "GT", "BE", "MOE", "B", "MT")
COUNTED = {
    "scores_ready": ("ST",), "weights_ready": ("ST",), "attended": ("PV",), "head_out_ready": ("YE",),
    "swapped": ("ROPE",), "rotated": ("ROPE",), "parts_ready": ("SPLIT",), "parts_stored": ("SPLIT",),
    "values_copied": ("VCOPY",), "maxima_ready": ("MT",), "maxrows_ready": ("MT",),
    "stats_ready": ("N1", "N2"), "normed": ("N1A", "N2A"), "hi_ready": ("ZT",),
    "shifted": ("GA",), "gate_exp": ("GA",), "gates_ready": ("GB",),
    "stored": ("N2A",),
}
LINKS = {
    "SPLIT": 3, "YT": 1, "WO": 2, "N1": 12, "N2": 14, "MT": 2, "GA": 3, "GB": 4, "MOE": 1,
}


def banks():
    out = {}
    for seg in ("mid", "pre"):
        steps = [s for s in plan(seg) if s[0] in BANKED]
        for n, step in enumerate(steps):
            out["pre" if seg == "pre" else "run", step] = n % NB
    return out


BANK = banks()


def bank(seg, step):
    return BANK["pre" if seg == "pre" else "run", step]


def ledger():
    book = {}

    def add(name, seg, step):
        book.setdefault((name, seg), []).append(step)

    for seg in SEGMENTS:
        for step in plan(seg):
            for name, kinds in COUNTED.items():
                if step[0] in kinds:
                    add(name, seg, step)
            if step[0] in BANKED:
                add(f"bank{bank(seg, step)}", seg, step)
            if step[0] == "LOAD":
                add(f"stack{stack_of(seg, step)}", seg, step)
            if step[0] == "MT":
                add(f"maxrow{stack_of(seg, step)}", seg, step)
            if step[0] == "XL":
                add(f"x_loaded{step[1] % 2}", seg, step)
            for _ in range(LINKS.get(step[0], 0)):
                add("link", seg, step)
            if step[0] == "XR":
                add(f"resid_loaded{step[1]}", seg, step)
            if step[0] == "ROPE":
                add("turning", seg, step)
    return book


def stack_of(seg, step):
    kind, s = step[:2]
    if seg == "pre" or kind == "ST":
        return s
    return (s + {"LOAD": 3, "B": 2, "MT": 2}[kind]) % SLOTS


BOOK = ledger()


class Count:

    def __init__(self, seg, turn=None):
        self.seg, self.turn = seg, turn

    def from_start(self, name, offset, per=1):
        n = offset
        for seg in SEGMENTS[:SEGMENTS.index(self.seg)]:
            n += len(BOOK.get((name, seg), ())) * (NMID if seg == "mid" else 1)
        stride = len(BOOK.get((name, self.seg), ())) * per
        return self.turn * stride + n * per if self.seg == "mid" else n * per

    def at(self, name, step, per=1):
        here = BOOK[name, self.seg]
        return self.from_start(name, len(here) - here[::-1].index(step), per)

    def below(self, name, step, back=1, per=1):
        here = BOOK[name, self.seg]
        return self.from_start(name, here.index(step) + 1 - back, per)

    def so_far(self, name, step, per=1):
        n = 0
        for other in plan(self.seg):
            if other == step:
                break
            n += other in BOOK.get((name, self.seg), ())
        return self.from_start(name, n, per)

    def prev(self, name, step, per=1):
        before = SEGMENTS[:SEGMENTS.index(self.seg)]
        offsets = []
        for order in (before, before + ("mid",)) if self.seg == "mid" else (before,):
            back = 0
            for seg in reversed(order):
                steps = BOOK.get((name, seg), ())
                if step in steps:
                    offsets.append(-back - steps[::-1].index(step))
                    break
                back += len(steps)
        assert offsets and len(set(offsets)) == 1, (self.seg, name, step, offsets)
        return self.from_start(name, offsets[0], per)


def attention_moe_kernel(nc, x, w_qkv, w_o, w_gate, b_gate, w_exp, b_exp, rot_cos, rot_sin, out):
    x_d = x.rearrange("b (t p) d -> b p t d", p=P)
    out_d = out.rearrange("b (t p) d -> b p t d", p=P)
    scratch = nc.dram_tensor("parts_scratch", [2, 3, NH, DH, T], BF16).ap()

    with ExitStack() as ctx:
        def sb(name, shape, dt=F32):
            return ctx.enter_context(nc.sbuf_tensor(name, shape, dt))

        def sem(name):
            return ctx.enter_context(nc.semaphore(name))

        wqkv = sb("wqkv_sb", [P, KT, 3 * D])
        wo = sb("wo_sb", [P, KT, D])
        wexp_hi = sb("wexp_hi", [P, KT, NE * D], F32R)
        wexp_lo = sb("wexp_lo", [P, KT, NE * D], F32R)
        wgate = sb("wgate_sb", [P, KT, NE])
        wgate_hi = sb("wgate_hi", [P, KT, P], F32R)
        wgate_lo = sb("wgate_lo", [P, KT, P], F32R)
        bgate = sb("bgate_sb", [P, 1])
        cos = sb("cos_sb", [P, T])
        sin = sb("sin_sb", [P, T])
        ident = sb("ident", [P, P])
        ident_bf = sb("ident_bf", [P, P], BF16)
        far_qk = sb("far_qk", [P, P], BF16)
        far_kq = sb("far_kq", [P, P], BF16)
        x_in = sb("x_in", [P, 2, 2, D])
        xT = sb("xT", [P, KT, T])
        rope = sb("rope", [P, 2, CH])
        rope_swap = sb("rope_swap", [P, CH])
        parts = sb("parts", [P, 3, CH], BF16)
        q_stack = sb("q_stack", [P, SLOTS, QUAD, T], BF16)
        k_stack = sb("k_stack", [P, SLOTS, QUAD, T], BF16)
        v_next = sb("v_next", [P, SLOTS, VQ])
        v_now = sb("v_now", [P, SLOTS, VQ])
        maxima = sb("maxima", [P, 2, QUAD * TILES])
        maxima_hi = sb("maxima_hi", [P, 2, QUAD * TILES // 2])
        maxrow = sb("maxrow", [QUAD * TILES, 3, P], BF16)
        maxrow_err = sb("maxrow_err", [QUAD * TILES, P])
        weights = sb("weights", [P, 2, QUAD, CH])
        head_out = sb("head_out", [P, CH])
        sum_inv = sb("sum_inv", [P, 4 * QUAD])
        heads = sb("heads", [P, TILES, D])
        headsT = sb("headsT", [P, KT, CH])
        z = sb("z", [P, 2, 4, D])
        stats = sb("stats", [P, 4, 6])
        moments = sb("moments", [P, 2, 4, 2])
        newton = sb("newton", [P, 8, 4])
        newton_i = sb("newton_i", [P, 2, 4], I32)
        zT_hi = sb("zT_hi", [P, KT, CH], F32R)
        zT_lo = sb("zT_lo", [P, KT, CH], F32R)
        narrow = sb("narrow", [P, CH + D])
        logitsT = narrow[0:NE, 0:CH]
        gatesT, bexp = narrow[32:32 + NE, 0:CH], narrow[32:32 + NE, CH:CH + D]
        logits = sb("logits", [P, 4, 2 * NE])
        left = sb("left", [P, 4, 2 * NE])
        top = sb("top", [P, 4, NE])
        taken = sb("taken", [P, 4, NE])
        shift = sb("shift", [P, 4, NE])
        gate_e = sb("gate_e", [P, 4, NE])
        picked = sb("picked", [P, 4, NE])
        chosen = sb("chosen", [P, 4, NE])
        gate_sum = sb("gate_sum", [P, 2, 4])
        gates = sb("gates", [P, 4, NE])

        st = [ctx.enter_context(nc.psum_tensor(f"scores{i}", [P, 2, CH], F32)) for i in range(2)]
        pv = ctx.enter_context(nc.psum_tensor("attend", [P, CH], F32))
        bk = [ctx.enter_context(nc.psum_tensor(f"bank{i}", [P, CH], F32)) for i in range(NB)]

        names = [*COUNTED, "link", "turning", "sp_waits", "pool_waits", "dve_waits", "zeroed", "zeroed_v", "const_v", "const_p", "w_loaded", "hi_split", "w_split"]
        names += [f"{n}{i}" for n in ("stack", "maxrow") for i in range(SLOTS)]
        names += [f"{n}{i}" for n in ("x_loaded", "resid_loaded") for i in range(2)]
        S = {n: sem(n) for n in names}
        full = [sem(f"bank{i}_full") for i in range(NB)]
        free = [sem(f"bank{i}_free") for i in range(NB)]

        def v_heads(buf, s):
            return buf[:, s, 0:TILES * QUAD * VW].rearrange("p (b h v) -> p b h v", b=TILES, h=QUAD)

        def filled(eng, c, step):
            b = bank(c.seg, step)
            eng.wait_ge(full[b], c.at(f"bank{b}", step))

        def emptied(eng, c, step, prev=False):
            b = bank(c.seg, step)
            eng.wait_ge(free[b], (c.prev if prev else c.at)(f"bank{b}", step))

        def run(eng, work):
            for seg in SEGMENTS:
                batch = {"pre": 0, "first": 0, "last": B - 1, "post": B}.get(seg)
                if seg != "mid":
                    c = Count(seg)
                    for step in plan(seg):
                        work(c, batch, *step)
                    work(c, batch, "END")
                else:
                    with eng.Fori(0, NMID) as turn:
                        c = Count(seg, turn)
                        for step in plan(seg):
                            work(c, turn + 1, *step)
                        work(c, turn + 1, "END")

        block = ctx.enter_context(nc.Block())

        @block.sync
        def _(sp):
            for dst, src in ((wqkv[:, :, :], w_qkv.rearrange("(k p) n -> p k n", p=P)),
                             (wo[:, :, :], w_o.rearrange("(k p) n -> p k n", p=P)),
                             (cos[:, :], rot_cos), (sin[:, :], rot_sin),
                             (wgate[:, :, :], w_gate.rearrange("(k p) n -> p k n", p=P)),
                             (bexp[:, :], b_exp),
                             (bgate[0:NE, :], b_gate.rearrange("(n o) -> n o", o=1)),
                             (weights[:, 0, :, :], w_exp[0:P, :].rearrange("p (a n) -> p a n", a=4)),
                             (weights[:, 1, :, :], w_exp[P:2 * P, :].rearrange("p (a n) -> p a n", a=4))):
                sp.dma_start(dst, src).then_inc(S["w_loaded"], DMA)

            def wait_all(*waits):
                for n, (name, value) in enumerate(waits):
                    sp.wait_ge(S[name], value)
                    if n + 1 < len(waits):
                        sp.sem_inc(S["sp_waits"], 1)

            def work(c, batch, kind, *a):
                step = (kind, *a)
                if kind == "XL":
                    (j,) = a
                    if j >= 2:
                        emptied(sp, c, ("XT", j - 2))
                    nxt = batch if c.seg == "pre" else batch + 1
                    sp.dma_start(x_in[:, j % 2], x_d[nxt, :, 2 * j:2 * j + 2, :]) \
                      .then_inc(S[f"x_loaded{j % 2}"], DMA)
                elif kind == "SPLIT":
                    s, k = a
                    which, ch = k % 2, k // 2
                    waits = [("parts_ready", c.at("parts_ready", step))]
                    if c.seg != "pre" and k == 0:
                        waits += [(f"stack{n}", c.from_start(f"stack{n}", 0, LOADS)) for n in ((0, 1), (2,))[s]]
                        if s == 1:
                            waits.append(("stack3", c.at("stack3", ("LOAD", 0), LOADS)))
                    wait_all(*waits)
                    dst = scratch[which].rearrange("a h d t -> (h d) a t")
                    sp.dma_start(dst[s * P:(s + 1) * P, :, ch * CH:(ch + 1) * CH], parts[:, :, :]) \
                      .then_inc(S["parts_stored"], DMA)
                elif kind == "LOAD":
                    (s,) = a
                    n = stack_of(c.seg, step)
                    if c.seg != "pre" and s == 0:
                        waits = [("parts_stored", c.from_start("parts_stored", 0, DMA))]
                    else:
                        half = ((0, 0, 1) if c.seg == "pre" else (None, 0, 0, 1))[s]
                        waits = [("parts_stored", c.at("parts_stored", ("SPLIT", half, 3), DMA))]
                    if c.seg != "pre" and s > 0:
                        waits.append(("scores_ready", c.at("scores_ready", ("ST", ITEMS * s - 1, 1))))
                    elif c.seg in ("mid", "last"):
                        waits.append(("scores_ready", c.from_start("scores_ready", 0)))
                    wait_all(*waits)
                    for t, parts_qk in enumerate(TERMS):
                        for which, stack in enumerate((q_stack, k_stack)):
                            src = scratch[which, parts_qk[which], QUAD * n:QUAD * (n + 1)]
                            sp.dma_start(stack[DH * t:DH * (t + 1), n, :, :], src.rearrange("h d t -> d h t")) \
                              .then_inc(S[f"stack{n}"], DMA)
                elif kind == "MT":
                    n = stack_of(c.seg, step)
                    sp.wait_ge(S["maxrows_ready"], c.at("maxrows_ready", step))
                    for part in range(3):
                        dst = q_stack[ROWS + part:ROWS + part + 1, n, :, :]
                        sp.dma_start(dst.rearrange("o h (t q) -> o (h t) q", q=P), maxrow[:, part, :]) \
                          .then_inc(S[f"maxrow{n}"], DMA)
                elif kind == "XR":
                    (g,) = a
                    sp.dma_start(z[:, g], x_d[batch - 1, :, 4 * g:4 * g + 4, :]).then_inc(S[f"resid_loaded{g}"], DMA)
                elif kind == "N2A":
                    (g,) = a
                    sp.wait_ge(S["normed"], c.at("normed", step))
                    sp.dma_start(out_d[batch - 1, :, 4 * g:4 * g + 4, :], z[:, g]).then_inc(S["stored"], DMA)
                elif kind == "END" and ("stored", c.seg) in BOOK:
                    sp.wait_ge(S["stored"], c.at("stored", ("N2A", 1), DMA))
                    sp.sem_inc(S["sp_waits"], 1)

            run(sp, work)

        @block.gpsimd
        def _(pool):
            pool.memset(ident[:, :], 0.0).then_inc(S["zeroed"], 1)
            pool.memset(far_qk[:, :], 0.0).then_inc(S["zeroed"], 1)
            pool.memset(far_kq[:, :], 0.0).then_inc(S["zeroed"], 1)
            pool.memset(v_next[:, :, :], 1.0).then_inc(S["const_p"], 1)
            pool.memset(v_now[:, :, :], 1.0).then_inc(S["const_p"], 1)
            pool.wait_ge(S["zeroed"], 3)
            pool.affine_select(out=ident[:, :], in_=ident[:, :], compare_op=ALU.not_equal, fill=1.0, base=0,
                               pattern=[[-1, P]], channel_multiplier=1).then_inc(S["const_p"], 1)
            pool.affine_select(out=far_qk[:, :], in_=far_qk[:, :], compare_op=ALU.is_ge, fill=FAR, base=0,
                               pattern=[[-1, P]], channel_multiplier=1).then_inc(S["const_p"], 1)
            pool.affine_select(out=far_kq[:, :], in_=far_kq[:, :], compare_op=ALU.is_ge, fill=FAR, base=0,
                               pattern=[[1, P]], channel_multiplier=-1).then_inc(S["const_p"], 1)
            pool.wait_ge(S["w_loaded"], W_LOADS * DMA)
            pool.wait_ge(S["const_p"], CONST_P)

            def work(c, batch, kind, *a):
                step = (kind, *a)
                if kind == "ROPE":
                    s, k = a
                    x1, ch = rope[:, k % 2], k // 2
                    pool.wait_ge(S["swapped"], c.at("swapped", step))
                    pool.tensor_tensor(x1, x1, cos[:, ch * CH:(ch + 1) * CH], ALU.mult)
                    pool.tensor_tensor(rope_swap[:, :], rope_swap[:, :], sin[:, ch * CH:(ch + 1) * CH], ALU.mult) \
                        .then_inc(S["turning"], 1)
                    pool.wait_ge(S["turning"], c.at("turning", step))
                    pool.tensor_tensor(x1, x1, rope_swap[:, :], ALU.add).then_inc(S["rotated"], 1)
                elif kind == "VCOPY":
                    (s,) = a
                    if c.seg != "first" or s < SLOTS - 1:
                        if s < SLOTS - 1:
                            emptied(pool, c, ("VP", TILES // 2 - 1))
                        if c.seg != "pre":
                            pool.wait_ge(S["attended"], c.at("attended", ("PV", ITEMS * s + ITEMS - 1)))
                    pool.sem_inc(S["pool_waits"], 1)
                    pool.tensor_copy(v_heads(v_now, s), v_heads(v_next, s)).then_inc(S["values_copied"], 1)

            run(pool, work)

        @block.scalar
        def _(act):
            def work(c, batch, kind, *a):
                step = (kind, *a)
                b = bk[bank(c.seg, step)] if kind in BANKED else None
                fr = free[bank(c.seg, step)] if kind in BANKED else None
                if kind == "XT":
                    (j,) = a
                    filled(act, c, step)
                    act.activation(xT[:, :, 2 * P * j:2 * P * (j + 1)], b[:, :].rearrange("p (k n) -> p k n", k=KT),
                                   ACT.Copy).then_inc(fr, 1)
                elif kind == "QK":
                    s, k = a
                    filled(act, c, step)
                    if c.seg != "pre" or (s, k) > (0, 1):
                        act.wait_ge(S["parts_ready"], c.below("parts_ready", ("SPLIT", s, k), 2))
                    act.activation(rope[:, k % 2], b[:, :], ACT.Copy).then_inc(fr, 1)
                elif kind == "VP":
                    (j,) = a
                    filled(act, c, step)
                    if j == 0 and c.seg == "pre":
                        act.wait_ge(S["const_p"], CONST_P)
                    if j == 0 and c.seg != "pre":
                        act.wait_ge(S["values_copied"], c.at("values_copied", ("VCOPY", SLOTS - 1)))
                    for tt in range(2):
                        kb = 2 * j + tt
                        dst = v_next[:, :, kb * QUAD * VW:(kb + 1) * QUAD * VW]
                        last = act.activation(dst.rearrange("p s (h v) -> p s h v", h=QUAD)[:, :, :, 0:DH],
                                              b[:, tt * D:(tt + 1) * D].rearrange("p (s h v) -> p s h v", s=SLOTS, h=QUAD),
                                              ACT.Copy)
                    last.then_inc(fr, 1)
                elif kind == "ST":
                    n, p = a
                    kb, qc = ITEM[n % ITEMS]
                    c0 = score_width(kb, qc)
                    if c.seg == "first" and n == 0 and p == 0:
                        act.wait_ge(S["w_split"], 1)
                    act.wait_ge(S["scores_ready"], c.at("scores_ready", step))
                    if p == 0:
                        if n >= 2:
                            act.wait_ge(S["attended"], c.at("attended", ("PV", n - 2)))
                        elif c.seg != "first":
                            act.wait_ge(S["attended"], c.from_start("attended", n))
                    act.activation(weights[:, n % 2, 2 * p:2 * p + 2, c0:CH], st[p][:, :, c0:CH], ACT.Exp,
                                   scale=DH ** -0.5).then_inc(S["weights_ready"], 1)
                elif kind == "YE":
                    s, qc = a
                    act.wait_ge(S["attended"], c.at("attended", ("PV", ITEMS * s + (3, ITEMS - 1)[qc])))
                    if qc == 1:
                        if s < SLOTS - 1:
                            emptied(act, c, ("YT", s, 0))
                        elif c.seg == "post":
                            emptied(act, c, ("YT", s, 0), prev=True)
                        else:
                            emptied(act, c, LAST_B, prev=True)
                    elif s > 0:
                        emptied(act, c, ("YT", s - 1, 1))
                    elif c.seg != "first":
                        emptied(act, c, ("YT", SLOTS - 1, 1))
                    act.activation(head_out[:, :], pv[:, :], ACT.Copy).then_inc(S["head_out_ready"], 1)
                elif kind == "HT":
                    g, kt = a
                    filled(act, c, step)
                    if g:
                        emptied(act, c, ("WO", 0, 1))
                    act.activation(headsT[:, kt], b[:, :], ACT.Copy).then_inc(fr, 1)
                elif kind in ("N1A", "N2A"):
                    (g,) = a
                    act.wait_ge(S["stats_ready"], c.at("stats_ready", (kind[:2], g)))
                    for t in range(4):
                        last = act.activation(z[:, g, t], z[:, g, t], ACT.Identity, bias=newton[:, 7, t:t + 1],
                                              scale=newton[:, 6, t:t + 1])
                    last.then_inc(S["normed"], 1)
                elif kind == "ZT":
                    g, kt = a
                    filled(act, c, step)
                    if g:
                        emptied(act, c, ("MOE", 0, 3, NE // 2 - 1))
                    act.activation(zT_hi[:, kt], b[:, :], ACT.Copy).then_inc(S["hi_ready"], 1)
                elif kind == "GL":
                    filled(act, c, step)
                    act.activation(logitsT[:, :], b[0:NE, :], ACT.Identity, bias=bgate[0:NE, :]).then_inc(fr, 1)
                elif kind == "GA":
                    act.wait_ge(S["shifted"], c.at("shifted", step))
                    act.activation(gate_e[:, :, :], shift[:, :, :], ACT.Exp).then_inc(S["gate_exp"], 1)
                elif kind == "GT":
                    (g,) = a
                    filled(act, c, step)
                    if g:
                        emptied(act, c, ("BE", 0, 1))
                    act.activation(gatesT[:, :], b[0:NE, :], ACT.Copy).then_inc(fr, 1)

            act.wait_ge(S["w_loaded"], W_LOADS * DMA)
            run(act, work)

        @block.vector
        def _(dve):
            linked = [0]

            def link(c, step, ins):
                if linked[0] is None or linked[1:] != [c.seg, step]:
                    linked[:] = [0, c.seg, step]
                linked[0] += 1
                ins.then_inc(S["link"], 1)
                here = BOOK["link", c.seg]
                dve.wait_ge(S["link"], c.from_start("link", here.index(step) + linked[0]))

            def hold():
                dve.sem_inc(S["dve_waits"], 1)

            dve.memset(q_stack[:, :, :, :], 0.0).then_inc(S["zeroed_v"], 1)
            dve.memset(k_stack[:, :, :, :], 0.0).then_inc(S["zeroed_v"], 1)
            dve.memset(wgate_hi[:, :, :].bitcast(F32), 0.0).then_inc(S["zeroed_v"], 1)
            dve.memset(wgate_lo[:, :, :].bitcast(F32), 0.0).then_inc(S["zeroed_v"], 1)
            dve.memset(logits[:, :, NE:], SENTINEL).then_inc(S["const_v"], 1)
            dve.memset(taken[:, :, :], SENTINEL).then_inc(S["const_v"], 1)
            dve.wait_ge(S["zeroed_v"], 4)
            dve.memset(k_stack[ROWS:MROWS, :, :, :], 1.0).then_inc(S["const_v"], 1)
            dve.wait_ge(S["const_p"], CONST_P)
            dve.tensor_copy(ident_bf[:, :], ident[:, :]).then_inc(S["const_v"], 1)
            dve.wait_ge(S["w_loaded"], W_LOADS * DMA)
            for kt in range(KT):
                w = weights[:, kt].rearrange("p a n -> p (a n)")
                dve.tensor_copy(wexp_hi[:, kt], w).then_inc(S["hi_split"], 1)
                dve.tensor_copy(wgate_hi[:, kt, 0:NE], wgate[:, kt]).then_inc(S["hi_split"], 1)
            dve.wait_ge(S["hi_split"], 2 * KT)
            for kt in range(KT):
                w = weights[:, kt].rearrange("p a n -> p (a n)")
                dve.tensor_tensor(wexp_lo[:, kt], w, wexp_hi[:, kt].bitcast(F32), ALU.subtract)
                last = dve.tensor_tensor(wgate_lo[:, kt, 0:NE], wgate[:, kt], wgate_hi[:, kt, 0:NE].bitcast(F32),
                                         ALU.subtract)
            last.then_inc(S["w_split"], 1)
            dve.wait_ge(S["w_split"], 1)
            dve.wait_ge(S["const_v"], CONST_V)

            def rstd(c, step, g):
                v, y, t, u = newton[:, 0], newton[:, 1], newton[:, 2], newton[:, 3]
                link(c, step, dve.tensor_scalar(v, moments[:, g, :, 1], EPS, None, ALU.add))
                link(c, step, dve.tensor_scalar(newton_i[:, 0], v.bitcast(I32), 1, None, ALU.logical_shift_right))
                link(c, step, dve.tensor_scalar(y.bitcast(I32), newton_i[:, 0], -1.0, float(MAGIC), ALU.mult, ALU.add))
                for n in range(3):
                    link(c, step, dve.scalar_tensor_tensor(out=t, in0=y, scalar=-0.5, in1=y, op0=ALU.mult, op1=ALU.mult))
                    link(c, step, dve.tensor_tensor(u, t, v, ALU.mult))
                    dst = newton[:, 6] if n == 2 else newton[:, 4 + n]
                    link(c, step, dve.scalar_tensor_tensor(out=dst, in0=u, scalar=1.5, in1=y, op0=ALU.add, op1=ALU.mult))
                    y = dst
                dve.scalar_tensor_tensor(out=newton[:, 7], in0=moments[:, g, :, 0], scalar=-1.0, in1=newton[:, 6],
                                         op0=ALU.mult, op1=ALU.mult).then_inc(S["stats_ready"], 1)

            def work(c, batch, kind, *a):
                step = (kind, *a)
                b = bk[bank(c.seg, step)] if kind in BANKED else None
                fr = free[bank(c.seg, step)] if kind in BANKED else None
                if kind == "B":
                    s, it, hh = a
                    qt, kc = BITEM[it]
                    w = min(CH, P * (qt + 1) - CH * kc)
                    filled(dve, c, step)
                    dst = (maxima[:, s % 2, hh * TILES + qt:hh * TILES + qt + 1] if kc == 0 else
                           maxima_hi[:, s % 2, hh * 4 + qt - 4:hh * 4 + qt - 3])
                    dve.tensor_reduce(dst, b[:, 0:w], AX.X, ALU.max, negate=True).then_inc(fr, 1)
                elif kind == "MT":
                    (s,) = a
                    last_b = ("B", s, ITEMS - 1, QUAD - 1)
                    emptied(dve, c, last_b, prev=s == SLOTS - 1 and c.seg != "pre")
                    m = maxima[:, s % 2].rearrange("p (h t) -> p h t", h=QUAD)[:, :, 4:TILES]
                    dve.tensor_tensor(m, m, maxima_hi[:, s % 2].rearrange("p (h t) -> p h t", h=QUAD), ALU.min) \
                        .then_inc(S["maxima_ready"], 1)
                    filled(dve, c, step)
                    n = (stack_of(c.seg, step) - 1) % SLOTS
                    if c.seg != "pre" or s > 0:
                        dve.wait_ge(S[f"maxrow{n}"], c.so_far(f"maxrow{n}", step, 3 * DMA))
                    src = b[0:QUAD * TILES, 0:P]
                    link(c, step, dve.tensor_copy(maxrow[:, 0], src))
                    dve.tensor_tensor(maxrow_err[:, :], src, maxrow[:, 0], ALU.subtract).then_inc(fr, 1)
                    emptied(dve, c, step)
                    link(c, step, dve.tensor_copy(maxrow[:, 1], maxrow_err[:, :]))
                    dve.tensor_tensor(maxrow[:, 2], maxrow_err[:, :], maxrow[:, 1], ALU.subtract) \
                        .then_inc(S["maxrows_ready"], 1)
                elif kind == "ROPE":
                    s, k = a
                    emptied(dve, c, ("QK", s, k))
                    if c.seg != "pre" or (s, k) > (0, 0):
                        dve.wait_ge(S["rotated"], c.below("rotated", step, 1))
                    hold()
                    dve.stream_shuffle(rope_swap[:, :], rope[:, k % 2], SWAP).then_inc(S["swapped"], 1)
                elif kind == "SPLIT":
                    s, k = a
                    x1 = rope[:, k % 2]
                    dve.wait_ge(S["rotated"], c.at("rotated", ("ROPE", s, k)))
                    if c.seg != "pre" or (s, k) > (0, 0):
                        dve.wait_ge(S["parts_stored"], c.below("parts_stored", step, 1, DMA))
                    link(c, step, dve.tensor_copy(parts[:, 0], x1))
                    link(c, step, dve.tensor_tensor(x1, x1, parts[:, 0], ALU.subtract))
                    link(c, step, dve.tensor_copy(parts[:, 1], x1))
                    dve.tensor_tensor(parts[:, 2], x1, parts[:, 1], ALU.subtract).then_inc(S["parts_ready"], 1)
                elif kind == "YT":
                    s, qc = a
                    filled(dve, c, step)
                    src = b[:, :].rearrange("p (t j r) -> p t j r", t=4, j=QUAD)
                    inv = sum_inv[:, :].rearrange("p (t j) -> p t j", t=4)
                    link(c, step, dve.reciprocal(inv, src[:, :, :, DH]))
                    if s == 0 and qc == 0 and c.seg != "first":
                        emptied(dve, c, ("HT", 1, 1))
                    dst = heads[:, 4 * qc:4 * qc + 4, s * QUAD * DH:(s + 1) * QUAD * DH]
                    dve.tensor_tensor(dst.rearrange("p t (j d) -> p t j d", j=QUAD), src[:, :, :, 0:DH],
                                      inv.unsqueeze(3).to_broadcast([P, 4, QUAD, DH]), ALU.mult).then_inc(fr, 1)
                elif kind == "WO":
                    g, tp = a
                    filled(dve, c, step)
                    if tp == 0:
                        dve.wait_ge(S[f"resid_loaded{g}"], c.at(f"resid_loaded{g}", ("XR", g), DMA))
                    zz = z[:, g, 2 * tp:2 * tp + 2]
                    dve.tensor_tensor(zz, b[:, :].rearrange("p (t d) -> p t d", t=2), zz, ALU.add).then_inc(fr, 1)
                    emptied(dve, c, step)
                    dve.bn_stats(stats[:, 2 * tp], z[:, g, 2 * tp])
                    link(c, step, dve.bn_stats(stats[:, 2 * tp + 1], z[:, g, 2 * tp + 1]))
                    hold()
                    dve.bn_aggr(moments[:, g, 2 * tp], stats[:, 2 * tp])
                    link(c, step, dve.bn_aggr(moments[:, g, 2 * tp + 1], stats[:, 2 * tp + 1]))
                elif kind == "N1":
                    (g,) = a
                    if g:
                        dve.wait_ge(S["normed"], c.at("normed", ("N1A", 0)))
                    rstd(c, step, g)
                elif kind == "ZT":
                    g, kt = a
                    dve.wait_ge(S["hi_ready"], c.at("hi_ready", step))
                    dve.tensor_tensor(zT_lo[:, kt], b[:, :], zT_hi[:, kt].bitcast(F32), ALU.subtract).then_inc(fr, 1)
                elif kind == "GLT":
                    filled(dve, c, step)
                    dve.tensor_copy(logits[:, :, 0:NE], b[:, 0:4 * NE].rearrange("p (t e) -> p t e", t=4)).then_inc(fr, 1)
                elif kind == "GA":
                    (g,) = a
                    emptied(dve, c, ("GLT", g))
                    hold()
                    for t in range(3):
                        dve.max(top[:, t], logits[:, t, 0:NE])
                    link(c, step, dve.max(top[:, 3], logits[:, 3, 0:NE]))
                    dve.tensor_tensor(shift[:, :, :], logits[:, :, 0:NE], top[:, :, 0:1].to_broadcast([P, 4, NE]),
                                      ALU.subtract).then_inc(S["shifted"], 1)
                    link(c, step, dve.tensor_copy(taken[:, :, 0:2], top[:, :, 0:2]))
                    hold()
                    for t in range(3):
                        dve.match_replace(left[:, t], taken[:, t], logits[:, t], -SENTINEL)
                    link(c, step, dve.match_replace(left[:, 3], taken[:, 3], logits[:, 3], -SENTINEL))
                elif kind == "GB":
                    link(c, step, dve.tensor_tensor(picked[:, :, :], left[:, :, 0:NE], logits[:, :, 0:NE], ALU.not_equal))
                    dve.wait_ge(S["gate_exp"], c.at("gate_exp", ("GA", a[0])))
                    link(c, step, dve.tensor_tensor(chosen[:, :, :], gate_e[:, :, :], picked[:, :, :], ALU.mult))
                    link(c, step, dve.tensor_reduce(gate_sum[:, 0], chosen[:, :, :], AX.X, ALU.add))
                    link(c, step, dve.reciprocal(gate_sum[:, 1], gate_sum[:, 0]))
                    dve.tensor_tensor(gates[:, :, :], chosen[:, :, :],
                                      gate_sum[:, 1].unsqueeze(2).to_broadcast([P, 4, NE]), ALU.mult) \
                        .then_inc(S["gates_ready"], 1)
                elif kind == "BE":
                    g, tp = a
                    filled(dve, c, step)
                    zz = z[:, g, 2 * tp:2 * tp + 2]
                    dve.tensor_tensor(zz, b[:, :].rearrange("p (t d) -> p t d", t=2), zz, ALU.add).then_inc(fr, 1)
                elif kind == "MOE":
                    g, t, ch = a
                    filled(dve, c, step)
                    emptied(dve, c, ("BE", g, 1) if ch == 0 else ("MOE", g, t, ch - 1))
                    acc = z[:, g, t]
                    if t == 0 and ch == 0:
                        dve.wait_ge(S["gates_ready"], c.at("gates_ready", ("GB", g)))
                    link(c, step, dve.scalar_tensor_tensor(
                        out=acc, in0=b[:, 0:D], scalar=gates[:, t, 2 * ch:2 * ch + 1], in1=acc, op0=ALU.mult, op1=ALU.add))
                    dve.scalar_tensor_tensor(
                        out=acc, in0=b[:, D:2 * D], scalar=gates[:, t, 2 * ch + 1:2 * ch + 2], in1=acc,
                        op0=ALU.mult, op1=ALU.add).then_inc(fr, 1)
                elif kind == "N2":
                    (g,) = a
                    emptied(dve, c, ("MOE", g, 3, NE // 2 - 1))
                    dve.wait_ge(S["normed"], c.below("normed", ("N2A", g), 1))
                    for t in range(3):
                        dve.bn_stats(stats[:, t], z[:, g, t])
                    link(c, step, dve.bn_stats(stats[:, 3], z[:, g, 3]))
                    hold()
                    for t in range(3):
                        dve.bn_aggr(moments[:, g, t], stats[:, t])
                    link(c, step, dve.bn_aggr(moments[:, g, 3], stats[:, 3]))
                    rstd(c, step, g)

            run(dve, work)

        @block.tensor
        def _(pe):
            pe.wait_ge(S["w_split"], 1)
            pe.wait_ge(S["const_v"], CONST_V)

            def split_matmul(dst, lhs, rhs):
                pairs = [(i, j, kt) for i, j in ((0, 0), (0, 1), (1, 0)) for kt in range(KT)]
                for i, j, kt in pairs:
                    last = pe.matmul(dst, lhs(i, kt), rhs(j, kt), start=(i, j, kt) == pairs[0],
                                     stop=(i, j, kt) == pairs[-1])
                return last

            def work(c, batch, kind, *a):
                step = (kind, *a)
                if kind in BANKED:
                    nb = bank(c.seg, step)
                    b, fu = bk[nb], full[nb]

                def room():
                    if c.seg != "pre" or BOOK[f"bank{nb}", "pre"].index(step) > 0:
                        pe.wait_ge(free[nb], c.below(f"bank{nb}", step, 1))

                if kind == "XT":
                    (j,) = a
                    pe.wait_ge(S[f"x_loaded{j % 2}"], c.at(f"x_loaded{j % 2}", ("XL", j), DMA))
                    room()
                    for kt in range(KT):
                        for tt in range(2):
                            last = pe.transpose(b[:, kt * 2 * P + tt * P:kt * 2 * P + (tt + 1) * P],
                                                x_in[:, j % 2, tt, kt * P:(kt + 1) * P], ident[:, :])
                    last.then_inc(fu, 1)
                elif kind == "QK":
                    s, k = a
                    which, ch = k % 2, k // 2
                    emptied(pe, c, ("XT", 2 * ch + 1))
                    room()
                    col = which * D + s * P
                    for kt in range(KT):
                        last = pe.matmul(b[:, :], wqkv[:, kt, col:col + P], xT[:, kt, ch * CH:(ch + 1) * CH],
                                         start=kt == 0, stop=kt == KT - 1)
                    last.then_inc(fu, 1)
                elif kind == "VP":
                    (j,) = a
                    room()
                    for tt in range(2):
                        t = 2 * j + tt
                        for kt in range(KT):
                            last = pe.matmul(b[:, tt * D:(tt + 1) * D], xT[:, kt, t * P:(t + 1) * P],
                                             wqkv[:, kt, 2 * D:3 * D], start=kt == 0, stop=kt == KT - 1)
                    last.then_inc(fu, 1)
                elif kind == "B":
                    s, it, hh = a
                    n = stack_of(c.seg, step)
                    qt, kc = BITEM[it]
                    w = min(CH, P * (qt + 1) - CH * kc)
                    if it == 0 and hh == 0:
                        pe.wait_ge(S[f"stack{n}"], c.so_far(f"stack{n}", step, LOADS))
                    room()
                    diagonal = qt // 4 == kc
                    last = pe.matmul(b[:, 0:w], q_stack[0:ROWS, n, hh, qt * P:(qt + 1) * P],
                                     k_stack[0:ROWS, n, hh, kc * CH:kc * CH + w], start=True, stop=not diagonal)
                    if diagonal:
                        last = pe.matmul(b[:, w - P:w], ident_bf[:, :], far_qk[:, :], start=False, stop=True)
                    last.then_inc(fu, 1)
                elif kind == "MT":
                    (s,) = a
                    pe.wait_ge(S["maxima_ready"], c.at("maxima_ready", step))
                    room()
                    pe.transpose(b[0:QUAD * TILES, 0:P], maxima[:, s % 2, :], ident[:, :]).then_inc(fu, 1)
                elif kind == "ST":
                    n, p = a
                    s, it = divmod(n, ITEMS)
                    kb, qc = ITEM[it]
                    c0 = score_width(kb, qc)
                    if it == 0 and p == 0:
                        pe.wait_ge(S[f"maxrow{s}"], c.so_far(f"maxrow{s}", step, 3 * DMA))
                    if c.seg != "first" or n > 0:
                        pe.wait_ge(S["weights_ready"], c.below("weights_ready", step, 2))
                    diagonal = kb * P >= qc * CH
                    for i in range(2):
                        hh = 2 * p + i
                        last = pe.matmul(st[p][:, i, c0:CH], k_stack[0:MROWS, s, hh, kb * P:(kb + 1) * P],
                                         q_stack[0:MROWS, s, hh, qc * CH + c0:(qc + 1) * CH], start=True, stop=not diagonal)
                        if diagonal:
                            last = pe.matmul(st[p][:, i, c0:c0 + P], ident_bf[:, :], far_kq[:, :], start=False, stop=True)
                    last.then_inc(S["scores_ready"], 1)
                elif kind == "PV":
                    (n,) = a
                    s, it = divmod(n, ITEMS)
                    kb, qc = ITEM[it]
                    c0 = score_width(kb, qc)
                    if it == 0:
                        pe.wait_ge(S["values_copied"], c.so_far("values_copied", step))
                    if kb == 0 and (c.seg != "first" or n > 0):
                        pe.wait_ge(S["head_out_ready"], c.so_far("head_out_ready", step))
                    here = ("ST", n, 1) in BOOK.get(("weights_ready", c.seg), ())
                    if n == SLOTS * ITEMS - 1:
                        pe.wait_ge(S["weights_ready"], c.from_start("weights_ready", 0))
                    else:
                        assert here
                        pe.wait_ge(S["weights_ready"], c.at("weights_ready", ("ST", n, 1)))
                    for j in range(QUAD):
                        o = (kb * QUAD + j) * VW
                        last = pe.matmul(pv[32 * j:32 * j + 32, c0:CH], v_now[:, s, o:o + 32],
                                         weights[:, n % 2, j, c0:CH], start=kb == 0, stop=kb == 4 * qc + 3)
                    last.then_inc(S["attended"], 1)
                elif kind == "YT":
                    s, qc = a
                    pe.wait_ge(S["head_out_ready"], c.at("head_out_ready", ("YE", s, qc)))
                    room()
                    for t in range(4):
                        last = pe.transpose(b[:, t * P:(t + 1) * P], head_out[:, t * P:(t + 1) * P], ident[:, :])
                    last.then_inc(fu, 1)
                elif kind == "HT":
                    g, kt = a
                    emptied(pe, c, ("YT", SLOTS - 1, 1))
                    room()
                    for t in range(4):
                        last = pe.transpose(b[:, t * P:(t + 1) * P], heads[:, 4 * g + t, kt * P:(kt + 1) * P], ident[:, :])
                    last.then_inc(fu, 1)
                elif kind == "WO":
                    g, tp = a
                    emptied(pe, c, ("HT", g, KT - 1))
                    room()
                    for tt in range(2):
                        t = 2 * tp + tt
                        for kt in range(KT):
                            last = pe.matmul(b[:, tt * D:(tt + 1) * D], headsT[:, kt, t * P:(t + 1) * P], wo[:, kt, :],
                                             start=kt == 0, stop=kt == KT - 1)
                    last.then_inc(fu, 1)
                elif kind == "ZT":
                    g, kt = a
                    pe.wait_ge(S["normed"], c.at("normed", ("N1A", g)))
                    room()
                    for t in range(4):
                        last = pe.transpose(b[:, t * P:(t + 1) * P], z[:, g, t, kt * P:(kt + 1) * P], ident[:, :])
                    last.then_inc(fu, 1)
                elif kind == "GL":
                    (g,) = a
                    emptied(pe, c, ("ZT", g, 0))
                    emptied(pe, c, ("ZT", g, 1))
                    room()
                    split_matmul(b[:, :], lambda i, kt: (wgate_hi, wgate_lo)[i][:, kt],
                                 lambda j, kt: (zT_hi, zT_lo)[j][:, kt]).then_inc(fu, 1)
                elif kind == "GLT":
                    (g,) = a
                    emptied(pe, c, ("GL", g))
                    room()
                    for t in range(4):
                        last = pe.matmul(b[:, t * NE:(t + 1) * NE], logitsT[:, t * P:(t + 1) * P], ident[0:NE, 0:NE],
                                         start=True, stop=True)
                    last.then_inc(fu, 1)
                elif kind == "GT":
                    (g,) = a
                    pe.wait_ge(S["gates_ready"], c.at("gates_ready", ("GB", g)))
                    room()
                    for t in range(4):
                        last = pe.transpose(b[0:NE, t * P:(t + 1) * P], gates[:, t], ident[:, :])
                    last.then_inc(fu, 1)
                elif kind == "BE":
                    g, tp = a
                    emptied(pe, c, ("GT", g))
                    room()
                    for tt in range(2):
                        t = 2 * tp + tt
                        last = pe.matmul(b[:, tt * D:(tt + 1) * D], gatesT[:, t * P:(t + 1) * P], bexp[:, :],
                                         start=True, stop=True)
                    last.then_inc(fu, 1)
                elif kind == "MOE":
                    g, t, ch = a
                    room()
                    split_matmul(b[:, :], lambda i, kt: (zT_hi, zT_lo)[i][:, kt, t * P:(t + 1) * P],
                                 lambda j, kt: (wexp_hi, wexp_lo)[j][:, kt, ch * CH:(ch + 1) * CH]).then_inc(fu, 1)

            run(pe, work)


def rotation_tables():
    half = DH // 2
    freqs = np.arange(half, dtype=np.float32) / np.float32(half)
    theta = (np.float32(1.0) / np.power(np.float32(10000.0), freqs)).astype(np.float32)
    angle = (np.arange(T, dtype=np.float32)[None, :] * theta[:, None]).astype(np.float32)
    c, s = np.cos(angle).astype(np.float32), np.sin(angle).astype(np.float32)
    return (np.ascontiguousarray(np.tile(np.concatenate([c, c]), (HALF, 1))),
            np.ascontiguousarray(np.tile(np.concatenate([-s, s]), (HALF, 1))))


def kernel(L0_attn_x, L0_attn_W_qkv, L0_attn_W_o, L0_ffn_Wg, L0_ffn_bg, L0_ffn_We, L0_ffn_be):
    import concourse.bacc as bacc
    from concourse.bass_utils import run_bass_kernel_spmd

    cos, sin = rotation_tables()
    arrays = {
        "x": np.ascontiguousarray(L0_attn_x), "w_qkv": np.ascontiguousarray(L0_attn_W_qkv),
        "w_o": np.ascontiguousarray(L0_attn_W_o), "w_gate": np.ascontiguousarray(L0_ffn_Wg),
        "b_gate": np.ascontiguousarray(L0_ffn_bg),
        "w_exp": np.ascontiguousarray(np.asarray(L0_ffn_We).transpose(2, 0, 1).reshape(D, NE * D)),
        "b_exp": np.ascontiguousarray(L0_ffn_be), "rot_cos": cos, "rot_sin": sin,
    }
    nc = bacc.Bacc("TRN2", target_bir_lowering=False, num_devices=1)
    args = [nc.dram_tensor(f"in_{n}", a.shape, mybir.dt.from_np(a.dtype), kind="ExternalInput").ap()
            for n, a in arrays.items()]
    out = nc.dram_tensor("out_0", (B, T, D), F32, kind="ExternalOutput").ap()
    attention_moe_kernel(nc, *args, out)
    result = run_bass_kernel_spmd(nc, [{f"in_{n}": a for n, a in arrays.items()}], core_ids=[0])
    return result.results[0]["out_0"]
```

```python
from contextlib import ExitStack

import numpy as np

import concourse.bass as bass
from concourse import mybir

F32 = mybir.dt.float32
F32R = mybir.dt.float32r
BF16 = mybir.dt.bfloat16
I32 = mybir.dt.int32
ALU = mybir.AluOpType
ACT = mybir.ActivationFunctionType
AX = mybir.AxisListType

P = 128
B, T, D = 16, 1024, 256
NH = 16
DH = D // NH
NE = 8
TILES = T // P
CH = 512
KT = D // P
QUAD = 4
SLOTS = NH // QUAD
ITEMS = 12
ITEM = [(kb, qc) for qc in range(T // CH) for kb in range(CH // P * (qc + 1))]
HALF = P // DH
TERMS = ((0, 0), (0, 1), (1, 0), (1, 1), (0, 2), (2, 0))
ROWS = len(TERMS) * DH
MROWS = ROWS + 3
VW = DH + 1
VQ = TILES * QUAD * VW + 32 - VW
EPS = 1e-5
FAR = -1e38
SENTINEL = 3e38
MAGIC = 0x5F3759DF
NB = 3
DMA = 16
BITEM = [(qt, kc) for kc in range(T // CH) for qt in range(CH // P * kc, TILES)]
LOADS = 2 * len(TERMS) * DMA
W_LOADS = 7
CONST_P, CONST_V = 4, 4
SWAP = [(i // DH) * DH + (i + DH // 2) % DH for i in range(32)]
LAST_B = ("B", SLOTS - 1, ITEMS - 1, QUAD - 1)


def score_width(kb, qc):
    return max(0, kb * P - qc * CH)


PE_WORK = {"XT": 2, "QK": 8, "VP": 8, "ST": 2, "PV": 4, "YT": 2, "HT": 2, "WO": 8, "ZT": 2, "GL": 6, "GLT": 1,
           "GT": 2, "BE": 4, "MOE": 6, "MT": 1}
RSTD_STEPS = 13
SEGMENTS = ("pre", "first", "mid", "last", "post")
NMID = B - 2


def item_work(n):
    kb, qc = ITEM[n % ITEMS]
    qt, kc = BITEM[n % ITEMS]
    return QUAD * (2 * (CH - score_width(kb, qc)) + min(CH, P * (qt + 1) - CH * kc)) / CH


def plan(seg):
    ahead = seg in ("pre", "first", "mid")
    attend = seg in ("first", "mid", "last")
    behind = seg in ("mid", "last", "post")
    at = [[] for _ in range(SLOTS * ITEMS)]

    if ahead and seg != "pre":
        at[0] += [("XL", 0), ("XL", 1)]
        at[2] += [("XT", 0), ("XL", 2), ("XT", 1), ("XL", 3)]
        at[3] += [("XT", 2), ("XT", 3)]
        for s in range(NH // HALF):
            for k in range(4):
                n = (4, 24)[s] + 3 * k
                at[n].append(("QK", s, k))
                at[n + 1].append(("ROPE", s, k))
                at[n + 3].append(("CAST", s, k, 0))
                at[n + 4].append(("CAST", s, k, 1))
        for j in range(TILES // 2):
            at[(15, 18, 21, 25)[j]].append(("VP", j))
        for s in range(SLOTS - 1):
            at[(27, 28, 38)[s]].append(("VCOPY", s))
    if seg == "first":
        at[5].append(("WSPLIT",))
    if attend:
        at[2].append(("VCOPY", SLOTS - 1))
    if behind:
        at[1].append(("YT", SLOTS - 1, 1))
        experts = []
        for g in range(2):
            at[2].append(("XR", g))
            at[(4, 7)[g]] += [("HT", g, kt) for kt in range(KT)]
            for tp in range(2):
                at[(5, 9)[g] + tp].append(("WO", g, tp))
            first, second = ((7, 11)[g], (30, 46)[g])
            for i in range(RSTD_STEPS):
                at[first + min(i // 4, 2)].append(("RS", 1, g, i))
                at[second + 1 + (min(i // 4, 2), 0)[g]].append(("RS", 2, g, i))
            at[first + 3].append(("N1A", g))
            at[second].append(("N2", g))
            at[second + (4, 1)[g]].append(("N2A", g))
            gate = (11, 29)[g]
            at[gate] += [("ZT", g, kt) for kt in range(KT)]
            at[gate + 1] += [("GL", g)]
            at[gate + 3] += [("GLT", g), ("GA", g)]
            at[gate + 4] += [("GB", g)]
            at[gate + 5] += [("GT", g)]
            at[gate + 6] += [("BE", g, tp) for tp in range(2)]
            moe0, moe1 = ((17, 29), (35, 46))[g]
            jobs = [("MOE", g, t, c) for t in range(4) for c in range(NE // 2)]
            experts.append((jobs, moe0, moe1))
    if attend:
        for s in range(SLOTS):
            at[ITEMS * s + 9].append(("YT", s, 0))
            if s + 1 < SLOTS:
                at[ITEMS * s + ITEMS + 1].append(("YT", s, 1))
    if behind:
        for jobs, moe0, moe1 in experts:
            load = {n: sum(PE_WORK.get(step[0], 0) for step in at[n]) + item_work(n) for n in range(moe0, moe1)}
            share = dict.fromkeys(load, 0)
            for _ in jobs:
                n = min(load, key=load.get)
                load[n] += PE_WORK["MOE"]
                share[n] += 1
            for n in sorted(share):
                at[n] += jobs[:share[n]]
                jobs = jobs[share[n]:]
    bslots = {"pre": (), "first": (0, 1, 2, 3), "mid": (0, 1, 2, 3), "last": (0, 1), "post": ()}[seg]
    for s in bslots:
        if s < SLOTS - 1:
            at[ITEMS * s + ITEMS].append(("MC", s))
            at[ITEMS * s + ITEMS + 2].append(("MT", s))
    if seg == "mid" or seg == "last":
        at[0].append(("MC", SLOTS - 1))
        at[2].append(("MT", SLOTS - 1))

    out = []
    if seg == "pre":
        out += [("XL", 0), ("XL", 1), ("XT", 0), ("XL", 2), ("XT", 1), ("XL", 3), ("XT", 2), ("XT", 3)]
        halves = [(s, k) for s in range(NH // HALF) for k in range(4)]
        scores = [("B", 0, it, hh) for it in range(ITEMS) for hh in range(QUAD)]
        for m in range(len(halves) + 1):
            if m < len(halves):
                out += [("QK", *halves[m]), ("ROPE", *halves[m])]
            if m:
                out += [("CAST", *halves[m - 1], n) for n in range(2)]
            if m == 4:
                out += [("LOAD", 0)]
            if m >= 5:
                out += [("VP", m - 5)]
            if m == 6:
                out += [("LOAD", 1)]
        out += [("VCOPY", s) for s in range(SLOTS - 1)]
        out += [("LOAD", 2)] + scores + [("MC", 0), ("MT", 0)]
        out += [("B", 1, it, hh) for it in range(ITEMS) for hh in range(QUAD)]
        out += [("MC", 1), ("MT", 1)]
        return out
    for n in range(SLOTS * ITEMS):
        s, it = divmod(n, ITEMS)
        row = []
        if attend:
            if it == (4, 6, 2, 2)[s] and (ahead or s == 0):
                row.append(("LOAD", s))
            row += [("ST", n, 0), ("ST", n, 1)]
        row += at[n]
        if attend and n:
            row += [("PV", n - 1)]
            if (n - 1) % ITEMS in (3, ITEMS - 1):
                row.append(("YE", (n - 1) // ITEMS, int((n - 1) % ITEMS != 3)))
        if n == 0 and behind:
            row += [("PV", SLOTS * ITEMS - 1), ("YE", SLOTS - 1, 1)]
        short = [step for step in row if step[0] == "RS"]
        last = [step for step in row if step[0] in ("N1A", "N2A")] if short else []
        row = [step for step in row if step not in short + last]
        marks = [PE_WORK.get(step[0], 0) for step in row]
        total, done, nb = sum(marks), 0, 0
        for step, mark in zip(row, marks):
            out.append(step)
            done += mark
            while attend and s in bslots and nb < QUAD and done * QUAD >= 1.15 * (nb + 0.1) * total:
                out += [("B", s, it, nb), *short[:1]]
                short = short[1:]
                nb += 1
        out += short + last
    return out


BANKED = ("XT", "QK", "VP", "YT", "HT", "WO", "ZT", "GL", "GLT", "GT", "BE", "MOE", "B", "MT")
COUNTED = {
    "scores_ready": ("ST",), "weights_ready": ("ST",), "attended": ("PV",), "head_out_ready": ("YE",),
    "swapped": ("ROPE",), "rotated": ("ROPE",), "cast": ("CAST",), 
    "values_copied": ("VCOPY",), "maxima_ready": ("MC",), "maxrows_ready": ("MT",),
    "summed": ("N2",), "root": ("RS",), "normed": ("N1A", "N2A"), "hi_ready": ("ZT",),
    "shifted": ("GA",), "gate_exp": ("GA",), "gates_ready": ("GB",),
    "stored": ("N2A",),
}
LINKS = {
    "YT": 1, "WO": 2, "N2": 1, "MT": 2, "GA": 3, "GB": 4, "MOE": 1,
}


def banks():
    out = {}
    for seg in ("mid", "pre"):
        steps = [s for s in plan(seg) if s[0] in BANKED]
        for n, step in enumerate(steps):
            out["pre" if seg == "pre" else "run", step] = n % NB
    return out


BANK = banks()


def bank(seg, step):
    return BANK["pre" if seg == "pre" else "run", step]


def ledger():
    book = {}

    def add(name, seg, step):
        book.setdefault((name, seg), []).append(step)

    for seg in SEGMENTS:
        for step in plan(seg):
            for name, kinds in COUNTED.items():
                if step[0] in kinds:
                    add(name, seg, step)
            if step[0] in BANKED:
                add(f"bank{bank(seg, step)}", seg, step)
            if step[0] == "LOAD":
                add(f"stack{stack_of(seg, step)}", seg, step)
            if step[0] == "MT":
                add(f"maxrow{stack_of(seg, step)}", seg, step)
            if step[0] == "XL":
                add(f"x_loaded{step[1] % 2}", seg, step)
            for _ in range(LINKS.get(step[0], 0)):
                add("link", seg, step)
            if step[0] == "XR":
                add(f"resid_loaded{step[1]}", seg, step)
            if step[0] == "CAST" and not step[3]:
                add("rest_ready", seg, step)
            if step[0] == "CAST" and step[3]:
                add("parts_ready", seg, step)
                add(f"parts_stored{step[2] % 2}", seg, step)
            if step[0] == "ROPE":
                add("turning", seg, step)
    return book


def stack_of(seg, step):
    kind, s = step[:2]
    if seg == "pre" or kind == "ST":
        return s
    return (s + {"LOAD": 3, "B": 2, "MT": 2}[kind]) % SLOTS


BOOK = ledger()


class Count:

    def __init__(self, seg, turn=None):
        self.seg, self.turn = seg, turn

    def from_start(self, name, offset, per=1):
        n = offset
        for seg in SEGMENTS[:SEGMENTS.index(self.seg)]:
            n += len(BOOK.get((name, seg), ())) * (NMID if seg == "mid" else 1)
        stride = len(BOOK.get((name, self.seg), ())) * per
        return self.turn * stride + n * per if self.seg == "mid" else n * per

    def at(self, name, step, per=1):
        here = BOOK[name, self.seg]
        return self.from_start(name, len(here) - here[::-1].index(step), per)

    def below(self, name, step, back=1, per=1):
        here = BOOK[name, self.seg]
        return self.from_start(name, here.index(step) + 1 - back, per)

    def so_far(self, name, step, per=1):
        n = 0
        for other in plan(self.seg):
            if other == step:
                break
            n += other in BOOK.get((name, self.seg), ())
        return self.from_start(name, n, per)

    def prev(self, name, step, per=1):
        before = SEGMENTS[:SEGMENTS.index(self.seg)]
        offsets = []
        for order in (before, before + ("mid",)) if self.seg == "mid" else (before,):
            back = 0
            for seg in reversed(order):
                steps = BOOK.get((name, seg), ())
                if step in steps:
                    offsets.append(-back - steps[::-1].index(step))
                    break
                back += len(steps)
        assert offsets and len(set(offsets)) == 1, (self.seg, name, step, offsets)
        return self.from_start(name, offsets[0], per)


def attention_moe_kernel(nc, x, w_qkv, w_o, w_gate, b_gate, w_exp, b_exp, rot_cos, rot_sin, out):
    x_d = x.rearrange("b (t p) d -> b p t d", p=P)
    out_d = out.rearrange("b (t p) d -> b p t d", p=P)
    scratch = nc.dram_tensor("parts_scratch", [2, 3, NH, DH, T], BF16).ap()

    with ExitStack() as ctx:
        def sb(name, shape, dt=F32):
            return ctx.enter_context(nc.sbuf_tensor(name, shape, dt))

        def sem(name):
            return ctx.enter_context(nc.semaphore(name))

        wqkv = sb("wqkv_sb", [P, KT, 3 * D])
        wo = sb("wo_sb", [P, KT, D])
        wexp_hi = sb("wexp_hi", [P, KT, NE * D], F32R)
        wexp_lo = sb("wexp_lo", [P, KT, NE * D], F32R)
        wgate = sb("wgate_sb", [P, KT, NE])
        wgate_hi = sb("wgate_hi", [P, KT, P], F32R)
        wgate_lo = sb("wgate_lo", [P, KT, P], F32R)
        bgate = sb("bgate_sb", [P, 1])
        cos = sb("cos_sb", [P, T])
        sin = sb("sin_sb", [P, T])
        ident = sb("ident", [P, P])
        ident_bf = sb("ident_bf", [P, P], BF16)
        far_q = sb("far_q", [P, CH])
        far_kq = sb("far_kq", [P, P], BF16)
        x_in = sb("x_in", [P, 2, 2, D])
        xT = sb("xT", [P, KT, T])
        rope = sb("rope", [P, 2, CH])
        rope_swap = sb("rope_swap", [P, CH])
        parts = sb("parts", [P, 2, 3, CH], BF16)
        q_stack = sb("q_stack", [P, SLOTS, QUAD, T], BF16)
        k_stack = sb("k_stack", [P, SLOTS, QUAD, T], BF16)
        v_next = sb("v_next", [P, SLOTS, VQ])
        v_now = sb("v_now", [P, SLOTS, VQ])
        maxima = sb("maxima", [P, 2, QUAD * TILES])
        maxima_hi = sb("maxima_hi", [P, 2, QUAD * TILES // 2])
        maxrow = sb("maxrow", [QUAD * TILES, 3, P], BF16)
        maxrow_err = sb("maxrow_err", [QUAD * TILES, P])
        weights = sb("weights", [P, 2, QUAD, CH])
        head_out = sb("head_out", [P, CH])
        sum_inv = sb("sum_inv", [P, 4 * QUAD])
        heads = sb("heads", [P, TILES, D])
        headsT = x_in.rearrange("p a t d -> p a (t d)")
        z = sb("z", [P, 2, 4, D])
        staged = [z.rearrange("p g t d -> p (g t d)"), heads.rearrange("p t d -> p (t d)")]
        stats = sb("stats", [P, 4, 6])
        moments = sb("moments", [P, 2, 4, 2])
        newton = sb("newton", [P, 8, 4])
        newton_i = sb("newton_i", [P, 2, 4], I32)
        zT_hi = sb("zT_hi", [P, KT, CH], F32R)
        zT_lo = sb("zT_lo", [P, KT, CH], F32R)
        narrow = sb("narrow", [P, CH + D])
        logitsT = narrow[0:NE, 0:CH]
        gatesT, bexp = narrow[32:32 + NE, 0:CH], narrow[32:32 + NE, CH:CH + D]
        logits = sb("logits", [P, 4, 2 * NE])
        left = sb("left", [P, 4, 2 * NE])
        top = sb("top", [P, 4, NE])
        taken = sb("taken", [P, 4, NE])
        shift = sb("shift", [P, 4, NE])
        gate_e = sb("gate_e", [P, 4, NE])
        picked = sb("picked", [P, 4, NE])
        chosen = sb("chosen", [P, 4, NE])
        gate_sum = sb("gate_sum", [P, 2, 4])
        gates = sb("gates", [P, 4, NE])

        st = [ctx.enter_context(nc.psum_tensor(f"scores{i}", [P, 2, CH], F32)) for i in range(2)]
        pv = ctx.enter_context(nc.psum_tensor("attend", [P, CH], F32))
        bk = [ctx.enter_context(nc.psum_tensor(f"bank{i}", [P, CH], F32)) for i in range(NB)]

        names = [*COUNTED, "link", "rest_ready", "parts_ready", "turning", "sp_waits", "pool_waits", "dve_waits",
                 "zeroed", "zeroed_v", "const_v", "const_p", "ident_ready", "w_loaded", "we_loaded", "hi_split", "w_split"]
        names += [f"{n}{i}" for n in ("stack", "maxrow") for i in range(SLOTS)]
        names += [f"{n}{i}" for n in ("x_loaded", "resid_loaded", "parts_stored") for i in range(2)]
        S = {n: sem(n) for n in names}
        full = [sem(f"bank{i}_full") for i in range(NB)]
        free = [sem(f"bank{i}_free") for i in range(NB)]

        def v_heads(buf, s):
            return buf[:, s, 0:TILES * QUAD * VW].rearrange("p (b h v) -> p b h v", b=TILES, h=QUAD)

        def filled(eng, c, step):
            b = bank(c.seg, step)
            eng.wait_ge(full[b], c.at(f"bank{b}", step))

        def emptied(eng, c, step, prev=False):
            b = bank(c.seg, step)
            eng.wait_ge(free[b], (c.prev if prev else c.at)(f"bank{b}", step))

        def run(eng, work):
            for seg in SEGMENTS:
                batch = {"pre": 0, "first": 0, "last": B - 1, "post": B}.get(seg)
                if seg != "mid":
                    c = Count(seg)
                    for step in plan(seg):
                        work(c, batch, *step)
                    work(c, batch, "END")
                else:
                    with eng.Fori(0, NMID) as turn:
                        c = Count(seg, turn)
                        for step in plan(seg):
                            work(c, turn + 1, *step)
                        work(c, turn + 1, "END")

        def rest(eng, c, s, k, n):
            x1 = rope[:, k % 2]
            eng.wait_ge(S["cast"], c.at("cast", ("CAST", s, k, n)))
            if n == 0:
                eng.tensor_tensor(x1, x1, parts[:, k % 2, 0], ALU.subtract).then_inc(S["rest_ready"], 1)
            else:
                eng.tensor_tensor(parts[:, k % 2, 2], x1, parts[:, k % 2, 1], ALU.subtract).then_inc(S["parts_ready"], 1)

        block = ctx.enter_context(nc.Block())

        @block.sync
        def _(sp):
            def wait_all(*waits):
                for n, (name, value) in enumerate(waits):
                    sp.wait_ge(S[name], value)
                    if n + 1 < len(waits):
                        sp.sem_inc(S["sp_waits"], 1)

            def work(c, batch, kind, *a):
                step = (kind, *a)
                if kind == "XL":
                    (j,) = a
                    if j >= 2:
                        emptied(sp, c, ("XT", j - 2))
                    nxt = batch if c.seg == "pre" else batch + 1
                    sp.dma_start(x_in[:, j % 2], x_d[nxt, :, 2 * j:2 * j + 2, :]) \
                      .then_inc(S[f"x_loaded{j % 2}"], DMA)
                elif kind == "CAST" and a[2]:
                    s, k, _ = a
                    which, ch = k % 2, k // 2
                    waits = [("parts_ready", c.at("parts_ready", step))]
                    if c.seg != "pre" and k == 0:
                        waits += [(f"stack{n}", c.from_start(f"stack{n}", 0, LOADS)) for n in ((0, 1), (2,))[s]]
                        if s == 1:
                            waits.append(("stack3", c.at("stack3", ("LOAD", 0), LOADS)))
                    wait_all(*waits)
                    dst = scratch[which].rearrange("a h d t -> (h d) a t")
                    sp.dma_start(dst[s * P:(s + 1) * P, :, ch * CH:(ch + 1) * CH], parts[:, k % 2]) \
                      .then_inc(S[f"parts_stored{k % 2}"], DMA)
                elif kind == "LOAD":
                    (s,) = a
                    n = stack_of(c.seg, step)
                    if c.seg != "pre" and s == 0:
                        waits = [(f"parts_stored{i}", c.from_start(f"parts_stored{i}", 0, DMA)) for i in range(2)]
                    else:
                        half = ((0, 0, 1) if c.seg == "pre" else (None, 0, 0, 1))[s]
                        waits = [(f"parts_stored{i}", c.at(f"parts_stored{i}", ("CAST", half, 2 + i, 1), DMA))
                                 for i in range(2)]
                    if c.seg != "pre" and s > 0:
                        waits.append(("scores_ready", c.at("scores_ready", ("ST", ITEMS * s - 1, 1))))
                    elif c.seg in ("mid", "last"):
                        waits.append(("scores_ready", c.from_start("scores_ready", 0)))
                    wait_all(*waits)
                    for t, parts_qk in enumerate(TERMS):
                        for which, stack in enumerate((q_stack, k_stack)):
                            src = scratch[which, parts_qk[which], QUAD * n:QUAD * (n + 1)]
                            sp.dma_start(stack[DH * t:DH * (t + 1), n, :, :], src.rearrange("h d t -> d h t")) \
                              .then_inc(S[f"stack{n}"], DMA)
                elif kind == "MT":
                    n = stack_of(c.seg, step)
                    sp.wait_ge(S["maxrows_ready"], c.at("maxrows_ready", step))
                    for part in range(3):
                        dst = q_stack[ROWS + part:ROWS + part + 1, n, :, :]
                        sp.dma_start(dst.rearrange("o h (t q) -> o (h t) q", q=P), maxrow[:, part, :]) \
                          .then_inc(S[f"maxrow{n}"], DMA)
                elif kind == "XR":
                    (g,) = a
                    sp.dma_start(z[:, g], x_d[batch - 1, :, 4 * g:4 * g + 4, :]).then_inc(S[f"resid_loaded{g}"], DMA)
                elif kind == "N2A":
                    (g,) = a
                    sp.wait_ge(S["normed"], c.at("normed", step))
                    sp.dma_start(out_d[batch - 1, :, 4 * g:4 * g + 4, :], z[:, g]).then_inc(S["stored"], DMA)
                elif kind == "END" and ("stored", c.seg) in BOOK:
                    sp.wait_ge(S["stored"], c.at("stored", ("N2A", 1), DMA))
                    sp.sem_inc(S["sp_waits"], 1)

            run(sp, work)

        @block.gpsimd
        def _(pool):
            for table in (ident[:, :], far_q[:, :], far_kq[:, :]):
                pool.memset(table, 0.0).then_inc(S["zeroed"], 1)
            pool.wait_ge(S["zeroed"], 3)
            pool.affine_select(out=ident[:, :], in_=ident[:, :], compare_op=ALU.not_equal, fill=1.0, base=0,
                               pattern=[[-1, P]], channel_multiplier=1).then_inc(S["ident_ready"], 1)
            pool.affine_select(out=far_q[:, CH - P:], in_=far_q[:, CH - P:], compare_op=ALU.is_ge, fill=FAR, base=0,
                               pattern=[[-1, P]], channel_multiplier=1).then_inc(S["const_p"], 1)
            pool.affine_select(out=far_kq[:, :], in_=far_kq[:, :], compare_op=ALU.is_ge, fill=FAR, base=0,
                               pattern=[[1, P]], channel_multiplier=-1).then_inc(S["const_p"], 1)
            pool.memset(v_next[:, :, :], 1.0).then_inc(S["const_p"], 1)
            pool.memset(v_now[:, :, :], 1.0).then_inc(S["const_p"], 1)
            pool.wait_ge(S["w_loaded"], W_LOADS * DMA)
            pool.wait_ge(S["const_p"], CONST_P)

            def work(c, batch, kind, *a):
                step = (kind, *a)
                if kind == "ROPE":
                    s, k = a
                    x1, ch = rope[:, k % 2], k // 2
                    pool.wait_ge(S["swapped"], c.at("swapped", step))
                    pool.tensor_tensor(x1, x1, cos[:, ch * CH:(ch + 1) * CH], ALU.mult)
                    pool.tensor_tensor(rope_swap[:, :], rope_swap[:, :], sin[:, ch * CH:(ch + 1) * CH], ALU.mult) \
                        .then_inc(S["turning"], 1)
                    pool.wait_ge(S["turning"], c.at("turning", step))
                    pool.tensor_tensor(x1, x1, rope_swap[:, :], ALU.add).then_inc(S["rotated"], 1)
                elif kind == "CAST" and c.seg != "pre":
                    rest(pool, c, *a)
                elif kind in ("N1A", "N2A"):
                    (g,) = a
                    pool.wait_ge(S["root"], c.at("root", ("RS", int(kind[1]), g, RSTD_STEPS - 1)))
                    pool.sem_inc(S["pool_waits"], 1)
                    for t in range(4):
                        last = pool.tensor_scalar(z[:, g, t], z[:, g, t], newton[:, 6, t:t + 1], newton[:, 7, t:t + 1],
                                                  ALU.mult, ALU.add)
                    last.then_inc(S["normed"], 1)
                elif kind == "VCOPY":
                    (s,) = a
                    if s < SLOTS - 1:
                        emptied(pool, c, ("VP", TILES // 2 - 1))
                    if c.seg != "pre" and (c.seg != "first" or s < SLOTS - 1):
                        pool.wait_ge(S["attended"], c.at("attended", ("PV", ITEMS * s + ITEMS - 1)))
                    pool.sem_inc(S["pool_waits"], 1)
                    pool.tensor_copy(v_heads(v_now, s), v_heads(v_next, s)).then_inc(S["values_copied"], 1)

            run(pool, work)

        @block.scalar
        def _(act):
            def work(c, batch, kind, *a):
                step = (kind, *a)
                b = bk[bank(c.seg, step)] if kind in BANKED else None
                fr = free[bank(c.seg, step)] if kind in BANKED else None
                if kind == "END" and c.seg == "pre":
                    for kt in range(KT):
                        act.dma_start(staged[kt], w_exp[kt * P:(kt + 1) * P, :]).then_inc(S["we_loaded"], DMA)
                elif kind == "XT":
                    (j,) = a
                    filled(act, c, step)
                    act.activation(xT[:, :, 2 * P * j:2 * P * (j + 1)], b[:, :].rearrange("p (k n) -> p k n", k=KT),
                                   ACT.Copy).then_inc(fr, 1)
                elif kind == "QK":
                    s, k = a
                    filled(act, c, step)
                    if c.seg != "pre" or (s, k) > (0, 1):
                        act.wait_ge(S["parts_ready"], c.below("parts_ready", ("CAST", s, k, 1), 2))
                    act.activation(rope[:, k % 2], b[:, :], ACT.Copy).then_inc(fr, 1)
                elif kind == "CAST":
                    s, k, n = a
                    if n:
                        act.wait_ge(S["rest_ready"], c.at("rest_ready", ("CAST", s, k, 0)))
                    else:
                        act.wait_ge(S["rotated"], c.at("rotated", ("ROPE", s, k)))
                        if c.seg != "pre" or (s, k) > (0, 1):
                            act.wait_ge(S[f"parts_stored{k % 2}"],
                                        c.below(f"parts_stored{k % 2}", ("CAST", s, k, 1), 1, DMA))
                    act.activation(parts[:, k % 2, n], rope[:, k % 2], ACT.Copy).then_inc(S["cast"], 1)
                elif kind == "VP":
                    (j,) = a
                    filled(act, c, step)
                    if j == 0 and c.seg == "pre":
                        act.wait_ge(S["const_p"], CONST_P)
                    if j == 0 and c.seg != "pre":
                        act.wait_ge(S["values_copied"], c.at("values_copied", ("VCOPY", SLOTS - 1)))
                    for tt in range(2):
                        kb = 2 * j + tt
                        dst = v_next[:, :, kb * QUAD * VW:(kb + 1) * QUAD * VW]
                        last = act.activation(dst.rearrange("p s (h v) -> p s h v", h=QUAD)[:, :, :, 0:DH],
                                              b[:, tt * D:(tt + 1) * D].rearrange("p (s h v) -> p s h v", s=SLOTS, h=QUAD),
                                              ACT.Copy)
                    last.then_inc(fr, 1)
                elif kind == "ST":
                    n, p = a
                    kb, qc = ITEM[n % ITEMS]
                    c0 = score_width(kb, qc)
                    act.wait_ge(S["scores_ready"], c.at("scores_ready", step))
                    if p == 0:
                        if n >= 2:
                            act.wait_ge(S["attended"], c.at("attended", ("PV", n - 2)))
                        elif c.seg != "first":
                            act.wait_ge(S["attended"], c.from_start("attended", n))
                    act.activation(weights[:, n % 2, 2 * p:2 * p + 2, c0:CH], st[p][:, :, c0:CH], ACT.Exp,
                                   scale=DH ** -0.5).then_inc(S["weights_ready"], 1)
                elif kind == "YE":
                    s, qc = a
                    act.wait_ge(S["attended"], c.at("attended", ("PV", ITEMS * s + (3, ITEMS - 1)[qc])))
                    if qc == 1:
                        if s < SLOTS - 1:
                            emptied(act, c, ("YT", s, 0))
                        elif c.seg == "post":
                            emptied(act, c, ("YT", s, 0), prev=True)
                        else:
                            emptied(act, c, LAST_B, prev=True)
                    elif s > 0:
                        emptied(act, c, ("YT", s - 1, 1))
                    elif c.seg != "first":
                        emptied(act, c, ("YT", SLOTS - 1, 1))
                    act.activation(head_out[:, :], pv[:, :], ACT.Copy).then_inc(S["head_out_ready"], 1)
                elif kind == "HT":
                    g, kt = a
                    filled(act, c, step)
                    if g:
                        emptied(act, c, ("WO", 0, 1))
                    act.activation(headsT[:, kt], b[:, :], ACT.Copy).then_inc(fr, 1)
                elif kind == "ZT":
                    g, kt = a
                    filled(act, c, step)
                    if g:
                        emptied(act, c, ("MOE", 0, 3, NE // 2 - 1))
                    act.activation(zT_hi[:, kt], b[:, :], ACT.Copy).then_inc(S["hi_ready"], 1)
                elif kind == "GL":
                    filled(act, c, step)
                    act.activation(logitsT[:, :], b[0:NE, :], ACT.Identity, bias=bgate[0:NE, :]).then_inc(fr, 1)
                elif kind == "GA":
                    act.wait_ge(S["shifted"], c.at("shifted", step))
                    act.activation(gate_e[:, :, :], shift[:, :, :], ACT.Exp).then_inc(S["gate_exp"], 1)
                elif kind == "GT":
                    (g,) = a
                    filled(act, c, step)
                    if g:
                        emptied(act, c, ("BE", 0, 1))
                    act.activation(gatesT[:, :], b[0:NE, :], ACT.Copy).then_inc(fr, 1)

            for dst, src in ((wqkv[:, :, :], w_qkv.rearrange("(k p) n -> p k n", p=P)),
                             (wo[:, :, :], w_o.rearrange("(k p) n -> p k n", p=P)),
                             (cos[:, :], rot_cos), (sin[:, :], rot_sin),
                             (wgate[:, :, :], w_gate.rearrange("(k p) n -> p k n", p=P)),
                             (bexp[:, :], b_exp),
                             (bgate[0:NE, :], b_gate.rearrange("(n o) -> n o", o=1))):
                act.dma_start(dst, src).then_inc(S["w_loaded"], DMA)
            act.wait_ge(S["w_loaded"], W_LOADS * DMA)
            run(act, work)

        @block.vector
        def _(dve):
            linked = [0, None, None]

            def link(c, step, ins):
                if linked[1:] != [c.seg, step]:
                    linked[:] = [0, c.seg, step]
                linked[0] += 1
                ins.then_inc(S["link"], 1)
                here = BOOK["link", c.seg]
                dve.wait_ge(S["link"], c.from_start("link", here.index(step) + linked[0]))

            def hold():
                dve.sem_inc(S["dve_waits"], 1)

            dve.memset(wgate_hi[:, :, :].bitcast(F32), 0.0).then_inc(S["zeroed_v"], 1)
            dve.memset(wgate_lo[:, :, :].bitcast(F32), 0.0).then_inc(S["zeroed_v"], 1)
            dve.memset(logits[:, :, NE:], SENTINEL).then_inc(S["const_v"], 1)
            dve.memset(taken[:, :, :], SENTINEL).then_inc(S["const_v"], 1)
            dve.memset(k_stack[ROWS:MROWS, :, :, :], -1.0).then_inc(S["const_v"], 1)
            dve.wait_ge(S["const_p"], CONST_P)
            dve.wait_ge(S["ident_ready"], 1)
            dve.tensor_copy(ident_bf[:, :], ident[:, :]).then_inc(S["const_v"], 1)
            dve.wait_ge(S["zeroed_v"], 2)
            dve.wait_ge(S["const_v"], CONST_V)

            def split_weights():
                dve.wait_ge(S["w_loaded"], W_LOADS * DMA)
                dve.wait_ge(S["we_loaded"], KT * DMA)
                for kt in range(KT):
                    w = staged[kt]
                    dve.tensor_copy(wexp_hi[:, kt], w).then_inc(S["hi_split"], 1)
                    dve.tensor_copy(wgate_hi[:, kt, 0:NE], wgate[:, kt]).then_inc(S["hi_split"], 1)
                dve.wait_ge(S["hi_split"], 2 * KT)
                for kt in range(KT):
                    w = staged[kt]
                    dve.tensor_tensor(wexp_lo[:, kt], w, wexp_hi[:, kt].bitcast(F32), ALU.subtract)
                    last = dve.tensor_tensor(wgate_lo[:, kt, 0:NE], wgate[:, kt], wgate_hi[:, kt, 0:NE].bitcast(F32),
                                             ALU.subtract)
                last.then_inc(S["w_split"], 1)
                dve.wait_ge(S["w_split"], 1)

            def rstd_step(g, i):
                v, t, u = newton[:, 0], newton[:, 2], newton[:, 3]
                ys = [newton[:, 1], newton[:, 4], newton[:, 5], newton[:, 6]]
                if i == 0:
                    return dve.tensor_scalar(v, moments[:, g, :, 1], EPS, None, ALU.add)
                if i == 1:
                    return dve.tensor_scalar(newton_i[:, 0], v.bitcast(I32), 1, None, ALU.logical_shift_right)
                if i == 2:
                    return dve.tensor_scalar(ys[0].bitcast(I32), newton_i[:, 0], -1.0, float(MAGIC), ALU.mult, ALU.add)
                if i == RSTD_STEPS - 1:
                    return dve.scalar_tensor_tensor(out=newton[:, 7], in0=moments[:, g, :, 0], scalar=-1.0, in1=ys[3],
                                                    op0=ALU.mult, op1=ALU.mult)
                n, part = divmod(i - 3, 3)
                if part == 0:
                    return dve.scalar_tensor_tensor(out=t, in0=ys[n], scalar=-0.5, in1=ys[n], op0=ALU.mult, op1=ALU.mult)
                if part == 1:
                    return dve.tensor_tensor(u, t, v, ALU.mult)
                return dve.scalar_tensor_tensor(out=ys[n + 1], in0=u, scalar=1.5, in1=ys[n], op0=ALU.add, op1=ALU.mult)

            def work(c, batch, kind, *a):
                step = (kind, *a)
                b = bk[bank(c.seg, step)] if kind in BANKED else None
                fr = free[bank(c.seg, step)] if kind in BANKED else None
                if kind == "B":
                    s, it, hh = a
                    qt, kc = BITEM[it]
                    w = min(CH, P * (qt + 1) - CH * kc)
                    filled(dve, c, step)
                    dst = (maxima[:, s % 2, hh * TILES + qt:hh * TILES + qt + 1] if kc == 0 else
                           maxima_hi[:, s % 2, hh * 4 + qt - 4:hh * 4 + qt - 3])
                    if qt // 4 == kc:
                        hold()
                        dve.tensor_tensor_reduce(out=b[:, 0:w], in0=b[:, 0:w], in1=far_q[:, CH - w:CH], scale=1.0,
                                                 scalar=-SENTINEL, op0=ALU.add, op1=ALU.max, accum_out=dst).then_inc(fr, 1)
                    else:
                        dve.tensor_reduce(dst, b[:, 0:w], AX.X, ALU.max).then_inc(fr, 1)
                elif kind == "MC":
                    (s,) = a
                    emptied(dve, c, ("B", s, ITEMS - 1, QUAD - 1), prev=s == SLOTS - 1 and c.seg != "pre")
                    m = maxima[:, s % 2].rearrange("p (h t) -> p h t", h=QUAD)[:, :, 4:TILES]
                    dve.tensor_tensor(m, m, maxima_hi[:, s % 2].rearrange("p (h t) -> p h t", h=QUAD), ALU.max) \
                        .then_inc(S["maxima_ready"], 1)
                elif kind == "MT":
                    (s,) = a
                    filled(dve, c, step)
                    n = (stack_of(c.seg, step) - 1) % SLOTS
                    if c.seg != "pre" or s > 0:
                        dve.wait_ge(S[f"maxrow{n}"], c.so_far(f"maxrow{n}", step, 3 * DMA))
                    src = b[0:QUAD * TILES, 0:P]
                    link(c, step, dve.tensor_copy(maxrow[:, 0], src))
                    dve.tensor_tensor(maxrow_err[:, :], src, maxrow[:, 0], ALU.subtract).then_inc(fr, 1)
                    emptied(dve, c, step)
                    link(c, step, dve.tensor_copy(maxrow[:, 1], maxrow_err[:, :]))
                    dve.tensor_tensor(maxrow[:, 2], maxrow_err[:, :], maxrow[:, 1], ALU.subtract) \
                        .then_inc(S["maxrows_ready"], 1)
                elif kind == "ROPE":
                    s, k = a
                    emptied(dve, c, ("QK", s, k))
                    if c.seg != "pre" or (s, k) > (0, 0):
                        dve.wait_ge(S["rotated"], c.below("rotated", step, 1))
                    hold()
                    dve.stream_shuffle(rope_swap[:, :], rope[:, k % 2], SWAP).then_inc(S["swapped"], 1)
                elif kind == "CAST" and c.seg == "pre":
                    rest(dve, c, *a)
                elif kind == "WSPLIT":
                    split_weights()
                elif kind == "YT":
                    s, qc = a
                    filled(dve, c, step)
                    src = b[:, :].rearrange("p (t j r) -> p t j r", t=4, j=QUAD)
                    inv = sum_inv[:, :].rearrange("p (t j) -> p t j", t=4)
                    link(c, step, dve.reciprocal(inv, src[:, :, :, DH]))
                    if s == 0 and qc == 0 and c.seg != "first":
                        emptied(dve, c, ("HT", 1, 1))
                    dst = heads[:, 4 * qc:4 * qc + 4, s * QUAD * DH:(s + 1) * QUAD * DH]
                    dve.tensor_tensor(dst.rearrange("p t (j d) -> p t j d", j=QUAD), src[:, :, :, 0:DH],
                                      inv.unsqueeze(3).to_broadcast([P, 4, QUAD, DH]), ALU.mult).then_inc(fr, 1)
                elif kind == "WO":
                    g, tp = a
                    filled(dve, c, step)
                    if tp == 0:
                        dve.wait_ge(S[f"resid_loaded{g}"], c.at(f"resid_loaded{g}", ("XR", g), DMA))
                    zz = z[:, g, 2 * tp:2 * tp + 2]
                    dve.tensor_tensor(zz, b[:, :].rearrange("p (t d) -> p t d", t=2), zz, ALU.add).then_inc(fr, 1)
                    emptied(dve, c, step)
                    dve.bn_stats(stats[:, 2 * tp], z[:, g, 2 * tp])
                    link(c, step, dve.bn_stats(stats[:, 2 * tp + 1], z[:, g, 2 * tp + 1]))
                    hold()
                    dve.bn_aggr(moments[:, g, 2 * tp], stats[:, 2 * tp])
                    link(c, step, dve.bn_aggr(moments[:, g, 2 * tp + 1], stats[:, 2 * tp + 1]))
                elif kind == "RS":
                    which, g, i = a
                    if i:
                        dve.wait_ge(S["root"], c.below("root", step, 1))
                    elif which == 2:
                        dve.wait_ge(S["summed"], c.at("summed", ("N2", g)))
                    if i == 0 and (which, g) != (1, 0):
                        dve.wait_ge(S["normed"], c.so_far("normed", step))
                    rstd_step(g, i).then_inc(S["root"], 1)
                elif kind == "ZT":
                    g, kt = a
                    dve.wait_ge(S["hi_ready"], c.at("hi_ready", step))
                    dve.tensor_tensor(zT_lo[:, kt], b[:, :], zT_hi[:, kt].bitcast(F32), ALU.subtract).then_inc(fr, 1)
                elif kind == "GLT":
                    filled(dve, c, step)
                    dve.tensor_copy(logits[:, :, 0:NE], b[:, 0:4 * NE].rearrange("p (t e) -> p t e", t=4)).then_inc(fr, 1)
                elif kind == "GA":
                    (g,) = a
                    emptied(dve, c, ("GLT", g))
                    hold()
                    for t in range(3):
                        dve.max(top[:, t], logits[:, t, 0:NE])
                    link(c, step, dve.max(top[:, 3], logits[:, 3, 0:NE]))
                    dve.tensor_tensor(shift[:, :, :], logits[:, :, 0:NE], top[:, :, 0:1].to_broadcast([P, 4, NE]),
                                      ALU.subtract).then_inc(S["shifted"], 1)
                    link(c, step, dve.tensor_copy(taken[:, :, 0:2], top[:, :, 0:2]))
                    hold()
                    for t in range(3):
                        dve.match_replace(left[:, t], taken[:, t], logits[:, t], -SENTINEL)
                    link(c, step, dve.match_replace(left[:, 3], taken[:, 3], logits[:, 3], -SENTINEL))
                elif kind == "GB":
                    link(c, step, dve.tensor_tensor(picked[:, :, :], left[:, :, 0:NE], logits[:, :, 0:NE], ALU.not_equal))
                    dve.wait_ge(S["gate_exp"], c.at("gate_exp", ("GA", a[0])))
                    link(c, step, dve.tensor_tensor(chosen[:, :, :], gate_e[:, :, :], picked[:, :, :], ALU.mult))
                    link(c, step, dve.tensor_reduce(gate_sum[:, 0], chosen[:, :, :], AX.X, ALU.add))
                    link(c, step, dve.reciprocal(gate_sum[:, 1], gate_sum[:, 0]))
                    dve.tensor_tensor(gates[:, :, :], chosen[:, :, :],
                                      gate_sum[:, 1].unsqueeze(2).to_broadcast([P, 4, NE]), ALU.mult) \
                        .then_inc(S["gates_ready"], 1)
                elif kind == "BE":
                    g, tp = a
                    filled(dve, c, step)
                    zz = z[:, g, 2 * tp:2 * tp + 2]
                    dve.tensor_tensor(zz, b[:, :].rearrange("p (t d) -> p t d", t=2), zz, ALU.add).then_inc(fr, 1)
                elif kind == "MOE":
                    g, t, ch = a
                    filled(dve, c, step)
                    emptied(dve, c, ("BE", g, 1) if ch == 0 else ("MOE", g, t, ch - 1))
                    acc = z[:, g, t]
                    if t == 0 and ch == 0:
                        dve.wait_ge(S["gates_ready"], c.at("gates_ready", ("GB", g)))
                    link(c, step, dve.scalar_tensor_tensor(
                        out=acc, in0=b[:, 0:D], scalar=gates[:, t, 2 * ch:2 * ch + 1], in1=acc, op0=ALU.mult, op1=ALU.add))
                    dve.scalar_tensor_tensor(
                        out=acc, in0=b[:, D:2 * D], scalar=gates[:, t, 2 * ch + 1:2 * ch + 2], in1=acc,
                        op0=ALU.mult, op1=ALU.add).then_inc(fr, 1)
                elif kind == "N2":
                    (g,) = a
                    emptied(dve, c, ("MOE", g, 3, NE // 2 - 1))
                    for t in range(3):
                        dve.bn_stats(stats[:, t], z[:, g, t])
                    link(c, step, dve.bn_stats(stats[:, 3], z[:, g, 3]))
                    hold()
                    for t in range(3):
                        dve.bn_aggr(moments[:, g, t], stats[:, t])
                    dve.bn_aggr(moments[:, g, 3], stats[:, 3]).then_inc(S["summed"], 1)

            run(dve, work)

        @block.tensor
        def _(pe):
            pe.wait_ge(S["ident_ready"], 1)

            def split_matmul(dst, lhs, rhs):
                pairs = [(i, j, kt) for i, j in ((0, 0), (0, 1), (1, 0)) for kt in range(KT)]
                for i, j, kt in pairs:
                    last = pe.matmul(dst, lhs(i, kt), rhs(j, kt), start=(i, j, kt) == pairs[0],
                                     stop=(i, j, kt) == pairs[-1])
                return last

            def work(c, batch, kind, *a):
                step = (kind, *a)
                if kind in BANKED:
                    nb = bank(c.seg, step)
                    b, fu = bk[nb], full[nb]

                def room():
                    if c.seg != "pre" or BOOK[f"bank{nb}", "pre"].index(step) > 0:
                        pe.wait_ge(free[nb], c.below(f"bank{nb}", step, 1))

                if kind == "END" and c.seg == "pre":
                    pe.wait_ge(S["const_v"], CONST_V)
                elif kind == "END" and c.seg == "first":
                    pe.wait_ge(S["w_split"], 1)
                elif kind == "XT":
                    (j,) = a
                    pe.wait_ge(S[f"x_loaded{j % 2}"], c.at(f"x_loaded{j % 2}", ("XL", j), DMA))
                    room()
                    for kt in range(KT):
                        for tt in range(2):
                            last = pe.transpose(b[:, kt * 2 * P + tt * P:kt * 2 * P + (tt + 1) * P],
                                                x_in[:, j % 2, tt, kt * P:(kt + 1) * P], ident[:, :])
                    last.then_inc(fu, 1)
                elif kind == "QK":
                    s, k = a
                    which, ch = k % 2, k // 2
                    if c.seg == "pre" and (s, k) == (0, 0):
                        pe.wait_ge(S["w_loaded"], W_LOADS * DMA)
                    emptied(pe, c, ("XT", 2 * ch + 1))
                    room()
                    col = which * D + s * P
                    for kt in range(KT):
                        last = pe.matmul(b[:, :], wqkv[:, kt, col:col + P], xT[:, kt, ch * CH:(ch + 1) * CH],
                                         start=kt == 0, stop=kt == KT - 1)
                    last.then_inc(fu, 1)
                elif kind == "VP":
                    (j,) = a
                    room()
                    for tt in range(2):
                        t = 2 * j + tt
                        for kt in range(KT):
                            last = pe.matmul(b[:, tt * D:(tt + 1) * D], xT[:, kt, t * P:(t + 1) * P],
                                             wqkv[:, kt, 2 * D:3 * D], start=kt == 0, stop=kt == KT - 1)
                    last.then_inc(fu, 1)
                elif kind == "B":
                    s, it, hh = a
                    n = stack_of(c.seg, step)
                    qt, kc = BITEM[it]
                    w = min(CH, P * (qt + 1) - CH * kc)
                    if it == 0 and hh == 0:
                        pe.wait_ge(S[f"stack{n}"], c.so_far(f"stack{n}", step, LOADS))
                    room()
                    pe.matmul(b[:, 0:w], q_stack[0:ROWS, n, hh, qt * P:(qt + 1) * P],
                              k_stack[0:ROWS, n, hh, kc * CH:kc * CH + w], start=True, stop=True).then_inc(fu, 1)
                elif kind == "MT":
                    (s,) = a
                    pe.wait_ge(S["maxima_ready"], c.at("maxima_ready", ("MC", s)))
                    room()
                    pe.transpose(b[0:QUAD * TILES, 0:P], maxima[:, s % 2, :], ident[:, :]).then_inc(fu, 1)
                elif kind == "ST":
                    n, p = a
                    s, it = divmod(n, ITEMS)
                    kb, qc = ITEM[it]
                    c0 = score_width(kb, qc)
                    if it == 0 and p == 0:
                        pe.wait_ge(S[f"maxrow{s}"], c.so_far(f"maxrow{s}", step, 3 * DMA))
                    if c.seg != "first" or n > 0:
                        pe.wait_ge(S["weights_ready"], c.below("weights_ready", step, 2))
                    diagonal = kb * P >= qc * CH
                    for i in range(2):
                        hh = 2 * p + i
                        last = pe.matmul(st[p][:, i, c0:CH], k_stack[0:MROWS, s, hh, kb * P:(kb + 1) * P],
                                         q_stack[0:MROWS, s, hh, qc * CH + c0:(qc + 1) * CH], start=True, stop=not diagonal)
                        if diagonal:
                            last = pe.matmul(st[p][:, i, c0:c0 + P], ident_bf[:, :], far_kq[:, :], start=False, stop=True)
                    last.then_inc(S["scores_ready"], 1)
                elif kind == "PV":
                    (n,) = a
                    s, it = divmod(n, ITEMS)
                    kb, qc = ITEM[it]
                    c0 = score_width(kb, qc)
                    if it == 0:
                        pe.wait_ge(S["values_copied"], c.so_far("values_copied", step))
                    if kb == 0 and (c.seg != "first" or n > 0):
                        pe.wait_ge(S["head_out_ready"], c.so_far("head_out_ready", step))
                    if n == SLOTS * ITEMS - 1:
                        pe.wait_ge(S["weights_ready"], c.from_start("weights_ready", 0))
                    else:
                        pe.wait_ge(S["weights_ready"], c.at("weights_ready", ("ST", n, 1)))
                    for j in range(QUAD):
                        o = (kb * QUAD + j) * VW
                        last = pe.matmul(pv[32 * j:32 * j + 32, c0:CH], v_now[:, s, o:o + 32],
                                         weights[:, n % 2, j, c0:CH], start=kb == 0, stop=kb == 4 * qc + 3)
                    last.then_inc(S["attended"], 1)
                elif kind == "YT":
                    s, qc = a
                    pe.wait_ge(S["head_out_ready"], c.at("head_out_ready", ("YE", s, qc)))
                    room()
                    for t in range(4):
                        last = pe.transpose(b[:, t * P:(t + 1) * P], head_out[:, t * P:(t + 1) * P], ident[:, :])
                    last.then_inc(fu, 1)
                elif kind == "HT":
                    g, kt = a
                    emptied(pe, c, ("YT", SLOTS - 1, 1))
                    room()
                    for t in range(4):
                        last = pe.transpose(b[:, t * P:(t + 1) * P], heads[:, 4 * g + t, kt * P:(kt + 1) * P], ident[:, :])
                    last.then_inc(fu, 1)
                elif kind == "WO":
                    g, tp = a
                    emptied(pe, c, ("HT", g, KT - 1))
                    room()
                    for tt in range(2):
                        t = 2 * tp + tt
                        for kt in range(KT):
                            last = pe.matmul(b[:, tt * D:(tt + 1) * D], headsT[:, kt, t * P:(t + 1) * P], wo[:, kt, :],
                                             start=kt == 0, stop=kt == KT - 1)
                    last.then_inc(fu, 1)
                elif kind == "ZT":
                    g, kt = a
                    pe.wait_ge(S["normed"], c.at("normed", ("N1A", g)))
                    room()
                    for t in range(4):
                        last = pe.transpose(b[:, t * P:(t + 1) * P], z[:, g, t, kt * P:(kt + 1) * P], ident[:, :])
                    last.then_inc(fu, 1)
                elif kind == "GL":
                    (g,) = a
                    emptied(pe, c, ("ZT", g, 0))
                    emptied(pe, c, ("ZT", g, 1))
                    room()
                    split_matmul(b[:, :], lambda i, kt: (wgate_hi, wgate_lo)[i][:, kt],
                                 lambda j, kt: (zT_hi, zT_lo)[j][:, kt]).then_inc(fu, 1)
                elif kind == "GLT":
                    (g,) = a
                    emptied(pe, c, ("GL", g))
                    room()
                    for t in range(4):
                        last = pe.matmul(b[:, t * NE:(t + 1) * NE], logitsT[:, t * P:(t + 1) * P], ident[0:NE, 0:NE],
                                         start=True, stop=True)
                    last.then_inc(fu, 1)
                elif kind == "GT":
                    (g,) = a
                    pe.wait_ge(S["gates_ready"], c.at("gates_ready", ("GB", g)))
                    room()
                    for t in range(4):
                        last = pe.transpose(b[0:NE, t * P:(t + 1) * P], gates[:, t], ident[:, :])
                    last.then_inc(fu, 1)
                elif kind == "BE":
                    g, tp = a
                    emptied(pe, c, ("GT", g))
                    room()
                    for tt in range(2):
                        t = 2 * tp + tt
                        last = pe.matmul(b[:, tt * D:(tt + 1) * D], gatesT[:, t * P:(t + 1) * P], bexp[:, :],
                                         start=True, stop=True)
                    last.then_inc(fu, 1)
                elif kind == "MOE":
                    g, t, ch = a
                    room()
                    split_matmul(b[:, :], lambda i, kt: (zT_hi, zT_lo)[i][:, kt, t * P:(t + 1) * P],
                                 lambda j, kt: (wexp_hi, wexp_lo)[j][:, kt, ch * CH:(ch + 1) * CH]).then_inc(fu, 1)

            run(pe, work)


def rotation_tables():
    half = DH // 2
    freqs = np.arange(half, dtype=np.float32) / np.float32(half)
    theta = (np.float32(1.0) / np.power(np.float32(10000.0), freqs)).astype(np.float32)
    angle = (np.arange(T, dtype=np.float32)[None, :] * theta[:, None]).astype(np.float32)
    c, s = np.cos(angle).astype(np.float32), np.sin(angle).astype(np.float32)
    return (np.ascontiguousarray(np.tile(np.concatenate([c, c]), (HALF, 1))),
            np.ascontiguousarray(np.tile(np.concatenate([-s, s]), (HALF, 1))))


def kernel(L0_attn_x, L0_attn_W_qkv, L0_attn_W_o, L0_ffn_Wg, L0_ffn_bg, L0_ffn_We, L0_ffn_be):
    import concourse.bacc as bacc
    from concourse.bass_utils import run_bass_kernel_spmd

    cos, sin = rotation_tables()
    arrays = {
        "x": np.ascontiguousarray(L0_attn_x), "w_qkv": np.ascontiguousarray(L0_attn_W_qkv),
        "w_o": np.ascontiguousarray(L0_attn_W_o), "w_gate": np.ascontiguousarray(L0_ffn_Wg),
        "b_gate": np.ascontiguousarray(L0_ffn_bg),
        "w_exp": np.ascontiguousarray(np.asarray(L0_ffn_We).transpose(2, 0, 1).reshape(D, NE * D)),
        "b_exp": np.ascontiguousarray(L0_ffn_be), "rot_cos": cos, "rot_sin": sin,
    }
    nc = bacc.Bacc("TRN2", target_bir_lowering=False, num_devices=1)
    args = [nc.dram_tensor(f"in_{n}", a.shape, mybir.dt.from_np(a.dtype), kind="ExternalInput").ap()
            for n, a in arrays.items()]
    out = nc.dram_tensor("out_0", (B, T, D), F32, kind="ExternalOutput").ap()
    attention_moe_kernel(nc, *args, out)
    result = run_bass_kernel_spmd(nc, [{f"in_{n}": a for n, a in arrays.items()}], core_ids=[0])
    return result.results[0]["out_0"]
```
